# Optimizing a Trainium2 kernel written in Bass

```python
import numpy as np
import jax
import jax.numpy as jnp

def _softmax(x, axis=-1):
    return jax.nn.softmax(x, axis=axis)

def _gelu(x):
    return jax.nn.gelu(x, approximate=True)

def _silu(x):
    return jax.nn.silu(x)

def _sigmoid(x):
    return jax.nn.sigmoid(x)

def _layernorm(x, axis=-1, eps=1e-05):
    m = jnp.mean(x, axis=axis, keepdims=True)
    v = jnp.var(x, axis=axis, keepdims=True)
    return (x - m) / jnp.sqrt(v + eps)

def _scatter_add(tgt, idx, src, axis=0):
    return tgt.at[idx].add(src)

def _segment_sum(src, seg, n):
    return jax.ops.segment_sum(src, seg, n)
kernel_name = 'mk_gps_d2_gnn_r8_55d169'

def setup_inputs(seed: int=0):
    np.random.seed(seed)
    _w = jnp.asarray

    def _rec_inputs():
        import jax
        import jax.numpy as jnp
        _gk = jax.random.key(seed)
        x = -8.776e-05 + 1 * jax.random.normal(jax.random.fold_in(_gk, 1), (1250, 512), jnp.float32)
        src = jax.random.randint(jax.random.fold_in(_gk, 2), (40000,), 0, 1250, jnp.int32)
        dst = jnp.minimum((1250 * jax.random.uniform(jax.random.fold_in(_gk, 3), (40000,)) ** 2.0).astype(jnp.int32), 9999)
        _o = jnp.argsort(dst, stable=True)
        src = src[_o]
        dst = dst[_o]
        return (x, src, dst)
    x, src, dst = _rec_inputs()

    def _L0_gnn_setup():
        import jax, jax.numpy as jnp
        import numpy as np

        def _mean_agg(h, src, dst, n):
            s = jax.ops.segment_sum(h[src], dst, num_segments=n)
            deg = jax.ops.segment_sum(jnp.ones((src.shape[0],), h.dtype), dst, num_segments=n)
            return s / jnp.maximum(deg, 1.0)[:, None]
        key = jax.random.key(seed)
        ks = jax.random.split(key, 7)
        N, E, D, H, L = (1250, 20000, 512, 512, 3)
        sc = 1.0 / np.sqrt(D)
        return {'feat': jax.random.normal(ks[0], (N, D), jnp.float32), 'src': jax.random.randint(ks[1], (E,), 0, N, jnp.int32), 'dst': jax.random.randint(ks[2], (E,), 0, N, jnp.int32), 'W_init': jax.random.normal(ks[3], (H, D), jnp.float32) * sc, 'W_fwd': jax.random.normal(ks[4], (L, H, H), jnp.float32) * sc, 'W_bwd': jax.random.normal(ks[5], (L, H, H), jnp.float32) * sc, 'W_self': jax.random.normal(ks[6], (L, H, 3 * H), jnp.float32) * (1.0 / np.sqrt(3 * H))}
    _L0_gnn_all = _L0_gnn_setup()
    _L0_gnn_in = {k: v for k, v in _L0_gnn_all.items() if k in ('W_init', 'W_fwd', 'W_bwd', 'W_self')}
    del _L0_gnn_all

    def _L0_mix_setup():
        import jax, jax.numpy as jnp
        import numpy as np
        DIM = 512
        H = 8
        C = 64
        HID = H * C
        NMEM = H

        def _rmsnorm_seq(x, w):
            n = jnp.sqrt(jnp.sum(x * x, axis=2, keepdims=True))
            return x / jnp.maximum(n, 1e-12) * w * jnp.asarray(DIM ** 0.5, x.dtype)
        key = jax.random.key(seed)
        ks = jax.random.split(key, 7)
        b, n = (4, 512)
        x = jax.random.normal(ks[0], (b, n, DIM), dtype=jnp.float32)
        norm_w = jnp.ones((1, 1, DIM), dtype=jnp.float32)
        w_qkv = jax.random.normal(ks[1], (DIM, 3 * HID), dtype=jnp.float32) / np.sqrt(DIM)
        mem_kv = jax.random.normal(ks[2], (2, H, C, NMEM), dtype=jnp.float32)
        w_out = jax.random.normal(ks[3], (HID, DIM), dtype=jnp.float32) / np.sqrt(HID)
        b_out = jax.random.normal(ks[4], (DIM,), dtype=jnp.float32) * 0.01
        out_norm_w = jnp.ones((1, 1, DIM), dtype=jnp.float32)
        return {'x': x, 'norm_w': norm_w, 'w_qkv': w_qkv, 'mem_kv': mem_kv, 'w_out': w_out, 'b_out': b_out, 'out_norm_w': out_norm_w}
    _L0_mix_all = _L0_mix_setup()
    _L0_mix_in = {k: v for k, v in _L0_mix_all.items() if k in ('norm_w', 'w_qkv', 'mem_kv', 'w_out', 'b_out', 'out_norm_w')}
    del _L0_mix_all

    def _L0_ffn_setup():
        import jax, jax.numpy as jnp
        import numpy as np
        ROUTER_JITTER = 0.01
        NEG_INF = -jnp.inf

        def _sparsemixer_eval(scores, num_experts):
            eids = jnp.arange(num_experts)
            max1 = jnp.max(scores, axis=-1, keepdims=True)
            sel1 = jnp.argmax(scores, axis=-1)
            factor1 = jnp.maximum(jnp.abs(scores), max1)
            mask1 = (max1 - scores) / factor1 > 2.0 * ROUTER_JITTER
            mg1 = jnp.where(mask1, NEG_INF, scores)
            p1 = jax.nn.softmax(mg1, axis=-1)
            mult1 = jnp.take_along_axis(p1, sel1[:, None], axis=-1)[:, 0]
            oh1 = sel1[:, None] == eids[None, :]
            masked_scores = jnp.where(oh1, NEG_INF, scores)
            max2 = jnp.max(masked_scores, axis=-1, keepdims=True)
            sel2 = jnp.argmax(masked_scores, axis=-1)
            factor2 = jnp.maximum(jnp.abs(scores), max2)
            mask2 = (max2 - scores) / factor2 > 2.0 * ROUTER_JITTER
            mg2 = jnp.where(mask2, NEG_INF, masked_scores)
            p2 = jax.nn.softmax(mg2, axis=-1)
            mult2 = jnp.take_along_axis(p2, sel2[:, None], axis=-1)[:, 0]
            weights = jnp.stack([mult1, mult2], axis=-1)
            experts = jnp.stack([sel1, sel2], axis=-1)
            return (weights, experts)
        B, S, H, F, E = (2, 256, 512, 1024, 8)
        key = jax.random.key(seed)
        ks = jax.random.split(key, 6)
        scale_h = 1.0 / np.sqrt(H)
        scale_f = 1.0 / np.sqrt(F)
        return {'x': jax.random.normal(ks[0], (B, S, H), dtype=jnp.float32), 'wg': jax.random.normal(ks[1], (H, E), dtype=jnp.float32) * scale_h, 'bg': jax.random.normal(ks[2], (E,), dtype=jnp.float32) * 0.01, 'w1': jax.random.normal(ks[3], (E, H, F), dtype=jnp.float32) * scale_h, 'w3': jax.random.normal(ks[4], (E, H, F), dtype=jnp.float32) * scale_h, 'w2': jax.random.normal(ks[5], (E, F, H), dtype=jnp.float32) * scale_f}
    _L0_ffn_all = _L0_ffn_setup()
    _L0_ffn_in = {k: v for k, v in _L0_ffn_all.items() if k in ('wg', 'bg', 'w1', 'w3', 'w2')}
    del _L0_ffn_all

    def _L1_gnn_setup():
        import jax, jax.numpy as jnp
        import numpy as np
        N, D, H, DK, DFF, DEG = (512, 512, 8, 64, 256, 64)
        E = N * DEG
        EPS = 1e-05

        def _ln(t, g, b):
            mu = t.mean(-1, keepdims=True)
            var = ((t - mu) ** 2).mean(-1, keepdims=True)
            return g * (t - mu) * jax.lax.rsqrt(var + EPS) + b
        key = jax.random.key(seed)
        ks = jax.random.split(key, 16)
        s = 1.0 / np.sqrt(D)
        sf = 1.0 / np.sqrt(DFF)
        return {'x': jax.random.normal(ks[0], (N, D), jnp.float32), 'src': jax.random.randint(ks[1], (E,), 0, N, dtype=jnp.int32), 'dst': jnp.repeat(jnp.arange(N, dtype=jnp.int32), DEG), 'Wq': jax.random.normal(ks[2], (D, D), jnp.float32) * s, 'bq': jnp.zeros((D,), jnp.float32), 'Wk': jax.random.normal(ks[3], (D, D), jnp.float32) * s, 'bk': jnp.zeros((D,), jnp.float32), 'Wv': jax.random.normal(ks[4], (D, D), jnp.float32) * s, 'bv': jnp.zeros((D,), jnp.float32), 'Wo': jax.random.normal(ks[5], (D, D), jnp.float32) * s, 'bo': jnp.zeros((D,), jnp.float32), 'g0': jnp.ones((D,), jnp.float32), 'b0': jnp.zeros((D,), jnp.float32), 'g1': jnp.ones((D,), jnp.float32), 'b1': jnp.zeros((D,), jnp.float32), 'W1': jax.random.normal(ks[6], (D, DFF), jnp.float32) * s, 'bf1': jnp.zeros((DFF,), jnp.float32), 'W2': jax.random.normal(ks[7], (DFF, D), jnp.float32) * sf, 'bf2': jnp.zeros((D,), jnp.float32), 'gn': jnp.ones((D,), jnp.float32), 'bn': jnp.zeros((D,), jnp.float32)}
    _L1_gnn_all = _L1_gnn_setup()
    _L1_gnn_in = {k: v for k, v in _L1_gnn_all.items() if k in ('Wq', 'bq', 'Wk', 'bk', 'Wv', 'bv', 'Wo', 'bo', 'g0', 'b0', 'g1', 'b1', 'W1', 'bf1', 'W2', 'bf2', 'gn', 'bn')}
    del _L1_gnn_all

    def _L1_mix_setup():
        import math
        import jax, jax.numpy as jnp
        import numpy as np
        NUM_HEADS = 8
        ALPHA = 20.0
        LN_EPS = 1e-05

        def _forward(x, qkv_w, qkv_b, ln_g, ln_b, out_w, out_b):
            B, N, C = x.shape
            H = NUM_HEADS
            D = C // H
            qkv = x @ qkv_w + qkv_b
            q, k, v = jnp.split(qkv, 3, axis=-1)

            def to_heads(t):
                return t.reshape(B, N, H, D).transpose(0, 2, 1, 3)
            q, k, v = (to_heads(q), to_heads(k), to_heads(v))
            q_norm = jnp.linalg.norm(q, axis=-1, keepdims=True)
            k_norm = jnp.linalg.norm(k, axis=-1, keepdims=True)
            q_t = q / q_norm
            dq = jnp.tanh(q / q_norm * ALPHA) * (math.pi / 4)
            dk = jnp.tanh(k / k_norm * ALPHA) * (math.pi / 4)
            k3 = jnp.abs(k) ** 3
            kf = jnp.concatenate([k3 * jnp.cos(dk), k3 * jnp.sin(dk)], axis=-1)
            power = 1.5 * (0.5 + jnp.tanh(q_norm))
            q_t = (q_t ** 2) ** power
            qf = jnp.concatenate([q_t * jnp.cos(dq), q_t * jnp.sin(dq)], axis=-1)
            k_mean = jnp.mean(kf, axis=2, keepdims=True)
            z = 1.0 / (jnp.einsum('bhnf,bhmf->bhnm', qf, k_mean) + 1e-06)
            scale = N ** (-0.5)
            kv = jnp.einsum('bhnf,bhnd->bhfd', kf * scale, v * scale)
            out = jnp.einsum('bhnf,bhfd->bhnd', qf, kv) * z
            out = out.transpose(0, 2, 1, 3).reshape(B, N, C)
            mu = jnp.mean(out, axis=-1, keepdims=True)
            var = jnp.var(out, axis=-1, keepdims=True)
            out = (out - mu) * jax.lax.rsqrt(var + LN_EPS) * ln_g + ln_b
            return out @ out_w + out_b
        key = jax.random.key(seed)
        ks = jax.random.split(key, 6)
        B, N, C = (8, 512, 512)
        s = 1.0 / math.sqrt(C)
        return {'x': jax.random.normal(ks[0], (B, N, C), dtype=jnp.float32), 'qkv_w': jax.random.normal(ks[1], (C, 3 * C), dtype=jnp.float32) * s, 'qkv_b': jnp.zeros((3 * C,), dtype=jnp.float32), 'ln_g': jnp.ones((C,), dtype=jnp.float32), 'ln_b': jnp.zeros((C,), dtype=jnp.float32), 'out_w': jax.random.normal(ks[2], (C, C), dtype=jnp.float32) * s, 'out_b': jnp.zeros((C,), dtype=jnp.float32)}
    _L1_mix_all = _L1_mix_setup()
    _L1_mix_in = {k: v for k, v in _L1_mix_all.items() if k in ('qkv_w', 'qkv_b', 'ln_g', 'ln_b', 'out_w', 'out_b')}
    del _L1_mix_all

    def _L1_ffn_setup():
        import jax, jax.numpy as jnp
        import numpy as np
        E = 8
        K = 1
        D = 512
        I = 256
        B, T = (2, 256)
        key = jax.random.key(seed)
        ks = jax.random.split(key, 7)
        s = 0.02
        x = jax.random.normal(ks[0], (B, T, D), jnp.float32)
        gate_w = jax.random.normal(ks[1], (E, D), jnp.float32) * s
        w1 = jax.random.normal(ks[2], (E, I, D), jnp.float32) * s
        w2 = jax.random.normal(ks[3], (E, D, I), jnp.float32) * s
        w3 = jax.random.normal(ks[4], (E, I, D), jnp.float32) * s
        sw1 = jax.random.normal(ks[5], (I, D), jnp.float32) * s
        sw2 = jax.random.normal(ks[6], (D, I), jnp.float32) * s
        return {'x': x, 'gate_w': gate_w, 'w1': w1, 'w2': w2, 'w3': w3, 'sw1': sw1, 'sw2': sw2}
    _L1_ffn_all = _L1_ffn_setup()
    _L1_ffn_in = {k: v for k, v in _L1_ffn_all.items() if k in ('gate_w', 'w1', 'w2', 'w3', 'sw1', 'sw2')}
    del _L1_ffn_all
    return {'x': x, 'src': src, 'dst': dst, 'L0_gnn_W_init': _L0_gnn_in['W_init'], 'L0_gnn_W_fwd': _L0_gnn_in['W_fwd'], 'L0_gnn_W_bwd': _L0_gnn_in['W_bwd'], 'L0_gnn_W_self': _L0_gnn_in['W_self'], 'L0_mix_norm_w': _L0_mix_in['norm_w'], 'L0_mix_w_qkv': _L0_mix_in['w_qkv'], 'L0_mix_mem_kv': _L0_mix_in['mem_kv'], 'L0_mix_w_out': _L0_mix_in['w_out'], 'L0_mix_b_out': _L0_mix_in['b_out'], 'L0_mix_out_norm_w': _L0_mix_in['out_norm_w'], 'L0_ffn_wg': _L0_ffn_in['wg'], 'L0_ffn_bg': _L0_ffn_in['bg'], 'L0_ffn_w1': _L0_ffn_in['w1'], 'L0_ffn_w3': _L0_ffn_in['w3'], 'L0_ffn_w2': _L0_ffn_in['w2'], 'L1_gnn_Wq': _L1_gnn_in['Wq'], 'L1_gnn_bq': _L1_gnn_in['bq'], 'L1_gnn_Wk': _L1_gnn_in['Wk'], 'L1_gnn_bk': _L1_gnn_in['bk'], 'L1_gnn_Wv': _L1_gnn_in['Wv'], 'L1_gnn_bv': _L1_gnn_in['bv'], 'L1_gnn_Wo': _L1_gnn_in['Wo'], 'L1_gnn_bo': _L1_gnn_in['bo'], 'L1_gnn_g0': _L1_gnn_in['g0'], 'L1_gnn_b0': _L1_gnn_in['b0'], 'L1_gnn_g1': _L1_gnn_in['g1'], 'L1_gnn_b1': _L1_gnn_in['b1'], 'L1_gnn_W1': _L1_gnn_in['W1'], 'L1_gnn_bf1': _L1_gnn_in['bf1'], 'L1_gnn_W2': _L1_gnn_in['W2'], 'L1_gnn_bf2': _L1_gnn_in['bf2'], 'L1_gnn_gn': _L1_gnn_in['gn'], 'L1_gnn_bn': _L1_gnn_in['bn'], 'L1_mix_qkv_w': _L1_mix_in['qkv_w'], 'L1_mix_qkv_b': _L1_mix_in['qkv_b'], 'L1_mix_ln_g': _L1_mix_in['ln_g'], 'L1_mix_ln_b': _L1_mix_in['ln_b'], 'L1_mix_out_w': _L1_mix_in['out_w'], 'L1_mix_out_b': _L1_mix_in['out_b'], 'L1_ffn_gate_w': _L1_ffn_in['gate_w'], 'L1_ffn_w1': _L1_ffn_in['w1'], 'L1_ffn_w2': _L1_ffn_in['w2'], 'L1_ffn_w3': _L1_ffn_in['w3'], 'L1_ffn_sw1': _L1_ffn_in['sw1'], 'L1_ffn_sw2': _L1_ffn_in['sw2']}

def reference(x, src, dst, L0_gnn_W_init, L0_gnn_W_fwd, L0_gnn_W_bwd, L0_gnn_W_self, L0_mix_norm_w, L0_mix_w_qkv, L0_mix_mem_kv, L0_mix_w_out, L0_mix_b_out, L0_mix_out_norm_w, L0_ffn_wg, L0_ffn_bg, L0_ffn_w1, L0_ffn_w3, L0_ffn_w2, L1_gnn_Wq, L1_gnn_bq, L1_gnn_Wk, L1_gnn_bk, L1_gnn_Wv, L1_gnn_bv, L1_gnn_Wo, L1_gnn_bo, L1_gnn_g0, L1_gnn_b0, L1_gnn_g1, L1_gnn_b1, L1_gnn_W1, L1_gnn_bf1, L1_gnn_W2, L1_gnn_bf2, L1_gnn_gn, L1_gnn_bn, L1_mix_qkv_w, L1_mix_qkv_b, L1_mix_ln_g, L1_mix_ln_b, L1_mix_out_w, L1_mix_out_b, L1_ffn_gate_w, L1_ffn_w1, L1_ffn_w2, L1_ffn_w3, L1_ffn_sw1, L1_ffn_sw2):
    import jax
    import jax.numpy as jnp

    def _L0_gnn_ref(feat, src, dst, W_init, W_fwd, W_bwd, W_self):
        import jax, jax.numpy as jnp
        import numpy as np

        def _mean_agg(h, src, dst, n):
            s = jax.ops.segment_sum(h[src], dst, num_segments=n)
            deg = jax.ops.segment_sum(jnp.ones((src.shape[0],), h.dtype), dst, num_segments=n)
            return s / jnp.maximum(deg, 1.0)[:, None]
        n = feat.shape[0]
        h = jax.nn.relu(feat @ W_init.T)
        num_layers = W_fwd.shape[0]
        for l in range(num_layers):
            h_self = h
            fwd_neigh = _mean_agg(h, src, dst, n) @ W_fwd[l].T
            bwd_neigh = _mean_agg(h, dst, src, n) @ W_bwd[l].T
            cat = jnp.concatenate((h_self, fwd_neigh, bwd_neigh), axis=1)
            h = jax.nn.relu(cat @ W_self[l].T)
        return h

    def _L0_mix_ref(x, norm_w, w_qkv, mem_kv, w_out, b_out, out_norm_w):
        import jax, jax.numpy as jnp
        import numpy as np
        DIM = 512
        H = 8
        C = 64
        HID = H * C
        NMEM = H

        def _rmsnorm_seq(x, w):
            n = jnp.sqrt(jnp.sum(x * x, axis=2, keepdims=True))
            return x / jnp.maximum(n, 1e-12) * w * jnp.asarray(DIM ** 0.5, x.dtype)
        b, n, _ = x.shape
        scale = jnp.asarray(C ** (-0.5), x.dtype)
        xn = _rmsnorm_seq(x, norm_w)
        qkv = xn @ w_qkv
        q, k, v = jnp.split(qkv, 3, axis=2)

        def to_heads(t):
            return t.reshape(b, n, H, C).transpose(0, 2, 3, 1)
        q, k, v = map(to_heads, (q, k, v))
        mk = jnp.broadcast_to(mem_kv[0], (b, H, C, NMEM))
        mv = jnp.broadcast_to(mem_kv[1], (b, H, C, NMEM))
        k = jnp.concatenate([mk, k], axis=-1)
        v = jnp.concatenate([mv, v], axis=-1)
        q = jax.nn.softmax(q, axis=-2) * scale
        k = jax.nn.softmax(k, axis=-1)
        context = jnp.einsum('bhdn,bhen->bhde', k, v)
        out = jnp.einsum('bhde,bhdn->bhen', context, q)
        out = out.transpose(0, 3, 1, 2).reshape(b, n, HID)
        out = out @ w_out + b_out
        return _rmsnorm_seq(out, out_norm_w)

    def _L0_ffn_ref(x, wg, bg, w1, w3, w2):
        import jax, jax.numpy as jnp
        import numpy as np
        ROUTER_JITTER = 0.01
        NEG_INF = -jnp.inf

        def _sparsemixer_eval(scores, num_experts):
            eids = jnp.arange(num_experts)
            max1 = jnp.max(scores, axis=-1, keepdims=True)
            sel1 = jnp.argmax(scores, axis=-1)
            factor1 = jnp.maximum(jnp.abs(scores), max1)
            mask1 = (max1 - scores) / factor1 > 2.0 * ROUTER_JITTER
            mg1 = jnp.where(mask1, NEG_INF, scores)
            p1 = jax.nn.softmax(mg1, axis=-1)
            mult1 = jnp.take_along_axis(p1, sel1[:, None], axis=-1)[:, 0]
            oh1 = sel1[:, None] == eids[None, :]
            masked_scores = jnp.where(oh1, NEG_INF, scores)
            max2 = jnp.max(masked_scores, axis=-1, keepdims=True)
            sel2 = jnp.argmax(masked_scores, axis=-1)
            factor2 = jnp.maximum(jnp.abs(scores), max2)
            mask2 = (max2 - scores) / factor2 > 2.0 * ROUTER_JITTER
            mg2 = jnp.where(mask2, NEG_INF, masked_scores)
            p2 = jax.nn.softmax(mg2, axis=-1)
            mult2 = jnp.take_along_axis(p2, sel2[:, None], axis=-1)[:, 0]
            weights = jnp.stack([mult1, mult2], axis=-1)
            experts = jnp.stack([sel1, sel2], axis=-1)
            return (weights, experts)
        B, S, H = x.shape
        E = w1.shape[0]
        xt = x.reshape(-1, H)
        scores = jax.nn.softmax(xt @ wg + bg, axis=-1)
        routing_weights, selected_experts = _sparsemixer_eval(scores, E)
        eids = jnp.arange(E)
        comb = jnp.sum(routing_weights[:, :, None] * (selected_experts[:, :, None] == eids[None, None, :]).astype(xt.dtype), axis=1)
        out = jnp.zeros_like(xt)
        for e in range(E):
            h = jax.nn.gelu(xt @ w1[e], approximate=False) * (xt @ w3[e])
            out = out + comb[:, e:e + 1] * (h @ w2[e])
        return out.reshape(B, S, H)

    def _L1_gnn_ref(x, src, dst, Wq, bq, Wk, bk, Wv, bv, Wo, bo, g0, b0, g1, b1, W1, bf1, W2, bf2, gn, bn):
        import jax, jax.numpy as jnp
        import numpy as np
        N, D, H, DK, DFF, DEG = (512, 512, 8, 64, 256, 64)
        E = N * DEG
        EPS = 1e-05

        def _ln(t, g, b):
            mu = t.mean(-1, keepdims=True)
            var = ((t - mu) ** 2).mean(-1, keepdims=True)
            return g * (t - mu) * jax.lax.rsqrt(var + EPS) + b
        n = x.shape[0]
        nx = _ln(x, g0, b0)
        q = (nx @ Wq + bq).reshape(n, H, DK)
        k = (nx @ Wk + bk).reshape(n, H, DK)
        v = (nx @ Wv + bv).reshape(n, H, DK)
        score = jnp.exp(jnp.clip(jnp.einsum('ehd,ehd->eh', k[src], q[dst]) / np.sqrt(DK), -5.0, 5.0))
        wv = jax.ops.segment_sum(score[:, :, None] * v[src], dst, num_segments=n)
        z = jax.ops.segment_sum(score, dst, num_segments=n)
        o = (wv / z[:, :, None]).reshape(n, H * DK) @ Wo + bo
        h1 = x + o
        ff = jax.nn.relu(_ln(h1, g1, b1) @ W1 + bf1) @ W2 + bf2
        h2 = h1 + ff
        return _ln(h2, gn, bn)

    def _L1_mix_ref(x, qkv_w, qkv_b, ln_g, ln_b, out_w, out_b):
        import math
        import jax, jax.numpy as jnp
        import numpy as np
        NUM_HEADS = 8
        ALPHA = 20.0
        LN_EPS = 1e-05

        def _forward(x, qkv_w, qkv_b, ln_g, ln_b, out_w, out_b):
            B, N, C = x.shape
            H = NUM_HEADS
            D = C // H
            qkv = x @ qkv_w + qkv_b
            q, k, v = jnp.split(qkv, 3, axis=-1)

            def to_heads(t):
                return t.reshape(B, N, H, D).transpose(0, 2, 1, 3)
            q, k, v = (to_heads(q), to_heads(k), to_heads(v))
            q_norm = jnp.linalg.norm(q, axis=-1, keepdims=True)
            k_norm = jnp.linalg.norm(k, axis=-1, keepdims=True)
            q_t = q / q_norm
            dq = jnp.tanh(q / q_norm * ALPHA) * (math.pi / 4)
            dk = jnp.tanh(k / k_norm * ALPHA) * (math.pi / 4)
            k3 = jnp.abs(k) ** 3
            kf = jnp.concatenate([k3 * jnp.cos(dk), k3 * jnp.sin(dk)], axis=-1)
            power = 1.5 * (0.5 + jnp.tanh(q_norm))
            q_t = (q_t ** 2) ** power
            qf = jnp.concatenate([q_t * jnp.cos(dq), q_t * jnp.sin(dq)], axis=-1)
            k_mean = jnp.mean(kf, axis=2, keepdims=True)
            z = 1.0 / (jnp.einsum('bhnf,bhmf->bhnm', qf, k_mean) + 1e-06)
            scale = N ** (-0.5)
            kv = jnp.einsum('bhnf,bhnd->bhfd', kf * scale, v * scale)
            out = jnp.einsum('bhnf,bhfd->bhnd', qf, kv) * z
            out = out.transpose(0, 2, 1, 3).reshape(B, N, C)
            mu = jnp.mean(out, axis=-1, keepdims=True)
            var = jnp.var(out, axis=-1, keepdims=True)
            out = (out - mu) * jax.lax.rsqrt(var + LN_EPS) * ln_g + ln_b
            return out @ out_w + out_b
        return _forward(x, qkv_w, qkv_b, ln_g, ln_b, out_w, out_b)

    def _L1_ffn_ref(x, gate_w, w1, w2, w3, sw1, sw2):
        import jax, jax.numpy as jnp
        import numpy as np
        E = 8
        K = 1
        D = 512
        I = 256
        B, T = (2, 256)
        xf = x.reshape(-1, D)
        logits = xf @ gate_w.T
        wts, idx = jax.lax.top_k(logits, K)
        wts = jax.nn.softmax(wts, axis=-1)
        comb = jnp.einsum('nke,nk->ne', jax.nn.one_hot(idx, E, dtype=xf.dtype), wts)
        h = jax.nn.silu(jnp.einsum('nd,eid->nei', xf, w1)) * jnp.einsum('nd,eid->nei', xf, w3)
        y = jnp.einsum('nei,edi->nd', h * comb[:, :, None], w2)
        y = y + jax.nn.gelu(xf @ sw1.T, approximate=False) @ sw2.T
        return y.reshape(x.shape)
    xn = _layernorm(x, axis=-1)
    x = x + _L0_gnn_ref(xn, src, dst, L0_gnn_W_init, L0_gnn_W_fwd, L0_gnn_W_bwd, L0_gnn_W_self) + _L0_mix_ref(xn[None], L0_mix_norm_w, L0_mix_w_qkv, L0_mix_mem_kv, L0_mix_w_out, L0_mix_b_out, L0_mix_out_norm_w)[0]
    x = x + _L0_ffn_ref(_layernorm(x, axis=-1)[None], L0_ffn_wg, L0_ffn_bg, L0_ffn_w1, L0_ffn_w3, L0_ffn_w2)[0]
    xn = _layernorm(x, axis=-1)
    x = x + _L1_gnn_ref(xn, src, dst, L1_gnn_Wq, L1_gnn_bq, L1_gnn_Wk, L1_gnn_bk, L1_gnn_Wv, L1_gnn_bv, L1_gnn_Wo, L1_gnn_bo, L1_gnn_g0, L1_gnn_b0, L1_gnn_g1, L1_gnn_b1, L1_gnn_W1, L1_gnn_bf1, L1_gnn_W2, L1_gnn_bf2, L1_gnn_gn, L1_gnn_bn) + _L1_mix_ref(xn[None], L1_mix_qkv_w, L1_mix_qkv_b, L1_mix_ln_g, L1_mix_ln_b, L1_mix_out_w, L1_mix_out_b)[0]
    x = x + _L1_ffn_ref(_layernorm(x, axis=-1)[None], L1_ffn_gate_w, L1_ffn_w1, L1_ffn_w2, L1_ffn_w3, L1_ffn_sw1, L1_ffn_sw2)[0]
    return x

_drawn_inputs = setup_inputs


def setup_inputs(seed=0):
    import zlib

    import numpy as np

    out = dict(_drawn_inputs(seed))
    spreads = {'L0_mix_norm_w': (1.0, 0.2),
     'L0_mix_out_norm_w': (1.0, 0.2),
     'L1_gnn_bq': (0.0, 0.8),
     'L1_gnn_bk': (0.0, 0.8),
     'L1_gnn_bv': (0.0, 0.278),
     'L1_gnn_bo': (0.0, 0.285),
     'L1_gnn_g0': (1.0, 0.2),
     'L1_gnn_b0': (0.0, 0.1),
     'L1_gnn_g1': (1.0, 0.2),
     'L1_gnn_b1': (0.0, 0.425),
     'L1_gnn_bf1': (0.0, 0.411),
     'L1_gnn_bf2': (0.0, 0.298),
     'L1_gnn_gn': (1.0, 0.2),
     'L1_gnn_bn': (0.0, 0.1),
     'L1_mix_qkv_b': (0.0, 0.1),
     'L1_mix_ln_g': (1.0, 0.2),
     'L1_mix_ln_b': (0.0, 0.1),
     'L1_mix_out_b': (0.0, 0.1)}
    factors = {'L1_ffn_gate_w': 4.371,
     'L1_ffn_w1': 4.444,
     'L1_ffn_w2': 4.415,
     'L1_ffn_w3': 4.377,
     'L1_ffn_sw1': 3.351,
     'L1_ffn_sw2': 3.222}
    for name, (base, spread) in spreads.items():
        noise = np.random.default_rng([zlib.crc32(name.encode()), seed]).standard_normal(out[name].shape)
        drawn = base * np.exp(spread * noise) if base else spread * noise
        out[name] = jnp.asarray(drawn.astype(out[name].dtype))
    for name, factor in factors.items():
        out[name] = (out[name] * factor).astype(out[name].dtype)
    return out
```

```python
import math
from contextlib import ExitStack

import concourse.bass as bass
from concourse import mybir

F32 = mybir.dt.float32
F32R = mybir.dt.float32r
BF16 = mybir.dt.bfloat16
F16 = mybir.dt.float16
I32 = mybir.dt.int32
ALU = mybir.AluOpType
ACT = mybir.ActivationFunctionType
AX = mybir.AxisListType.X

N = 1250
R = 125
T = N // R
D = 512
K = D // 128
EDGES = 40000
EG = 8
G = EDGES // (EG * R)
CH = [(0, 418), (418, 416), (834, 416)]


class Stage:

    def __init__(self, nc, name):
        self.nc, self.name, self.ctx = nc, name, ExitStack()
        self.sems = []

    def __enter__(self):
        self.ctx.__enter__()
        return self

    def __exit__(self, *a):
        return self.ctx.__exit__(*a)

    def sb(self, name, shape, dt=F32):
        return self.ctx.enter_context(self.nc.sbuf_tensor(f"{self.name}_{name}", shape, dt))

    def ps(self, name, shape, dt=F32):
        return self.ctx.enter_context(self.nc.psum_tensor(f"{self.name}_{name}", shape, dt))

    def sem(self, name):
        sem = self.ctx.enter_context(self.nc.semaphore(f"{self.name}_{name}"))
        self.sems.append(sem)
        return sem

    def kept_sem(self, name):
        return self.nc.alloc_semaphore(f"{self.name}_{name}")

    def clear(self):
        for sem in self.sems:
            self.nc.sync.sem_clear(sem)

    def block(self):
        self.ctx.callback(self.clear)
        return self.ctx.enter_context(self.nc.Block())


class Chain:

    def __init__(self, eng, sem, base=0):
        self.eng, self.sem, self.base, self.n = eng, sem, base, 0

    def __call__(self, ins):
        self.n += 1
        ins.then_inc(self.sem, 1)
        self.eng.wait_ge(self.sem, self.base + self.n)


def carry_wait(pool, c, carried, before):
    pool.wait_ge(carried, before)
    pool.tensor_tensor(c["spare"][:], c["ones"][0:1, 0:1], c["ones"][0:1, 0:1], ALU.add).then_inc(carried, 1)


def constants(nc, ctx):
    c = {}
    c["spare"] = ctx.enter_context(nc.sbuf_tensor("spare", [1, 1], F32))
    c["ident"] = ctx.enter_context(nc.sbuf_tensor("ident", [128, 128], F32))
    c["ident16"] = ctx.enter_context(nc.sbuf_tensor("ident16", [128, 128], BF16))
    c["ones"] = ctx.enter_context(nc.sbuf_tensor("ones", [128, 128], F32))
    c["ones16"] = ctx.enter_context(nc.sbuf_tensor("ones16", [128, 128], BF16))
    with Stage(nc, "const") as s:
        filled, made = s.sem("filled"), s.sem("made")
        block = s.block()

        @block.gpsimd
        def _(pool):
            pool.memset(c["ones"][:], 1.0).then_inc(filled, 1)
            pool.memset(c["ones16"][:], 1.0).then_inc(filled, 1)
            pool.memset(c["ident"][:], 0.0).then_inc(filled, 1)
            pool.memset(c["ident16"][:], 0.0).then_inc(filled, 1)
            pool.wait_ge(filled, 4)
            for name in ("ident", "ident16"):
                pool.affine_select(out=c[name][:], in_=c[name][:], compare_op=ALU.not_equal, fill=1.0,
                                   base=0, pattern=[[-1, 128]], channel_multiplier=1).then_inc(made, 1)
            pool.wait_ge(made, 2)
    return c


def stage_adjacency(nc, c, src_t, dst_t, dst_rows, table_dram, flag_dram, A, AT):
    W2 = 2 * R
    PASSES = 1 + T // 2
    DVE_K = 6
    ACT_K = EG - 1
    POOL_K = EG - DVE_K - 1
    NCH = len(CH)
    UNITS = 2 * NCH
    NG = PASSES * G
    with Stage(nc, "adj") as s:
        Af = s.sb("Af", [R, T, N])
        iota = s.sb("iota", [R, N], F16)
        iota_i = s.sb("iota_i", [R, N], I32)
        steps_i = s.sb("steps_i", [G, 8], I32)
        steps = s.sb("steps", [G, 8])
        src_i = s.sb("src_i", [R, G * EG], I32)
        dst_i = s.sb("dst_i", [R, G * EG], I32)
        rows_i = s.sb("rows_i", [G, EG * R], I32)
        rows_f = s.sb("rows_f", [G, EG * R])
        srcf = s.sb("srcf", [R, (G + 1) * EG])
        dstf = s.sb("dstf", [R, G * EG])
        rel = s.sb("rel", [R, PASSES * G * EG + EG])
        left = s.sb("left", [R, G * EG])
        far = s.sb("far", [R, G * EG])
        far1 = s.sb("far1", [R, 1])
        far_row = s.sb("far_row", [1, R])
        far_max = s.sb("far_max", [1, 1])
        far_flag = s.sb("far_flag", [1, 1], I32)
        gmin = s.sb("gmin", [G, 1])
        over = s.sb("over", [G, 8])
        base1 = s.sb("base1", [G, 2])
        gmax = s.sb("gmax", [G, 1])
        base_b = s.sb("base_b", [R, G])
        base_bs = s.sb("base_bs", [R, G])
        base_row = s.sb("base_row", [1, NG])
        pair_row = s.sb("pair_row", [1, NG])
        sums = s.sb("sums", [1, 2, NG])
        group_reg = s.sb("group_reg", [1, 3, NG], I32)
        oh_src = s.sb("oh_src", [R, 2, EG, N], BF16)
        oh_dst = s.sb("oh_dst", [R, 2, EG, W2], BF16)
        gap = s.sb("gap", [R, W2 + N], F16)
        less_rel = s.sb("less_rel", [R, PASSES * G * EG + EG])
        less_src = s.sb("less_src", [R, (G + 1) * EG])
        now_dst = s.sb("now_dst", [R, 2, POOL_K])
        now_src = s.sb("now_src", [R, 2, POOL_K])
        acc = s.ps("acc", [R, UNITS, 512])
        tr = s.ps("tr", [R, 2, 8, 128], BF16)

        loaded = s.sem("loaded")
        iotas = s.sem("iotas")
        base_out = s.sem("base_out")
        base_back = s.sem("base_back")
        far_in = s.sem("far_in")
        chain = s.sem("chain")
        flag_ready = s.sem("flag_ready")
        tables = s.sem("tables")
        oh_v = s.sem("oh_v")
        oh_p = s.sem("oh_p")
        unit_done = s.sem("unit_done")
        unit2_done = s.sem("unit2_done")
        bank_free = s.sem("bank_free")
        bank2_free = s.sem("bank2_free")
        a_bf = s.sem("a_bf")
        tr_done = s.sem("tr_done")
        tr_free = [s.sem(f"tr_free{b}") for b in range(2)]
        zeroed = s.sem("zeroed")
        oh_a = s.sem("oh_a")
        block = s.block()
        now = s.sem("now")
        gaps = s.sem("gaps")
        carried = s.sem("carried")

        def one_hot(p, g, b, k):
            e = p * (G * EG) + g * EG + k
            nc.vector.tensor_scalar(oh_dst[:, b, k, :], iota[:, 0:W2], rel[:, bass.ds(e, 1)], None, ALU.is_equal)
            return nc.vector.tensor_scalar(oh_src[:, b, k, :], iota[:], srcf[:, bass.ds(g * EG + k, 1)], None, ALU.is_equal)

        def turned_to(u):
            half, st = u // T, u % T
            return AT[:, st, half * 5 * R:(half + 1) * 5 * R].rearrange("p (j r) -> p j r", r=R)

        def second(eng, n):
            return (eng.value_load(group_reg[0:1, 1, bass.ds(n, 1)], min_val=0, max_val=1),
                    eng.value_load(group_reg[0:1, 2, bass.ds(n, 1)], min_val=0, max_val=NG))

        def wait_used(eng, n):
            before = eng.value_load(group_reg[0:1, 2, bass.ds(n - 1, 1)], min_val=0, max_val=NG)
            eng.wait_ge(unit_done, (n - 1) * NCH + 1)
            eng.wait_ge(unit2_done, before * NCH + 1)

        @block.sync
        def _(sp):
            sp.dma_start(src_i[:], src_t).then_inc(loaded, 16)
            sp.dma_start(dst_i[:], dst_t).then_inc(loaded, 16)
            sp.dma_start(rows_i[:], dst_rows).then_inc(loaded, 16)
            sp.wait_ge(base_out, 1)
            for i in range(2):
                sp.dma_start(table_dram[i].rearrange("(g a) -> g a", a=1), base1[:, i:i + 1]).then_inc(base_back, 16)
            sp.wait_ge(base_back, 32)
            for i, row in enumerate((base_row, pair_row)):
                sp.dma_start(row[:, 0:G], table_dram[i].rearrange("(a g) -> a g", a=1)).then_inc(base_back, 16)
            sp.dma_start(base_b[:], table_dram[0].partition_broadcast(R)).then_inc(base_back, 16)
            sp.wait_ge(far_in, 1)
            sp.dma_start(flag_dram[0:R].rearrange("(g a) -> g a", a=1), far1[:]).then_inc(far_in, 16)
            sp.wait_ge(far_in, 17)
            sp.dma_start(far_row[:], flag_dram[0:R].rearrange("(a g) -> a g", a=1)).then_inc(far_in, 16)
            sp.wait_ge(far_in, 33)

        @block.vector
        def _(dve):
            link = Chain(dve, chain)
            dve.wait_ge(iotas, 2)
            dve.wait_ge(loaded, 48)
            dve.memset(srcf[:, G * EG:], 0.0)
            dve.memset(rel[:, PASSES * G * EG:], 0.0)
            dve.tensor_copy(iota[:], iota_i[:])
            dve.tensor_copy(steps[:], steps_i[:])
            dve.tensor_copy(srcf[:, 0:G * EG], src_i[:])
            dve.tensor_copy(dstf[:], dst_i[:])
            link(dve.tensor_copy(rows_f[:], rows_i[:]))
            link(dve.tensor_reduce(gmin[:], rows_f[:], AX, ALU.min))
            link(dve.tensor_reduce(gmax[:], rows_f[:], AX, ALU.max))
            link(dve.tensor_scalar(over[:], steps[:], gmin[:, 0:1], None, ALU.is_le))
            link(dve.tensor_reduce(base1[:, 0:1], over[:], AX, ALU.add))
            link(dve.tensor_scalar(base1[:, 1:2], base1[:, 0:1], float(R), float(R), ALU.mult, ALU.add))
            link(dve.tensor_tensor(base1[:, 1:2], gmax[:], base1[:, 1:2], ALU.is_ge))
            dve.sem_inc(base_out, 1)
            dve.wait_ge(base_back, 80)
            for p in range(1, PASSES):
                dve.memset(base_row[:, p * G:(p + 1) * G], float(2 * (p - 1)))
            link(dve.memset(pair_row[:, G:], 1.0))
            link(dve.tensor_copy(sums[:, 0, :], pair_row[:]))
            step, now_in = 1, 0
            while step < NG:
                dve.tensor_copy(sums[:, 1 - now_in, 0:step], sums[:, now_in, 0:step])
                link(dve.tensor_tensor(sums[:, 1 - now_in, step:], sums[:, now_in, step:],
                                       sums[:, now_in, 0:NG - step], ALU.add))
                step, now_in = 2 * step, 1 - now_in
            link(dve.tensor_tensor(sums[:, now_in, :], sums[:, now_in, :], pair_row[:], ALU.subtract))
            link(dve.tensor_copy(group_reg[:, 1, :], pair_row[:]))
            link(dve.tensor_copy(group_reg[:, 2, :], sums[:, now_in, :]))
            link(dve.tensor_scalar(base_bs[:], base_b[:], float(R), None, ALU.mult))
            link(dve.tensor_copy(group_reg[:, 0, :], base_row[:]))
            link(dve.tensor_tensor(rel[:, 0:G * EG].rearrange("p (g k) -> p g k", k=EG),
                                   dstf[:].rearrange("p (g k) -> p g k", k=EG),
                                   base_bs[:].unsqueeze(2).to_broadcast([R, G, EG]), ALU.subtract))
            link(dve.tensor_scalar(far[:], rel[:, 0:G * EG], float(W2), None, ALU.is_ge))
            link(dve.tensor_reduce(far1[:], far[:], AX, ALU.max))
            dve.sem_inc(far_in, 1)
            link(dve.scalar_tensor_tensor(out=left[:], in0=dstf[:], scalar=-4095.0, in1=far[:],
                                          op0=ALU.add, op1=ALU.mult))
            for p in range(1, PASSES):
                link(dve.tensor_scalar(rel[:, p * G * EG:(p + 1) * G * EG], left[:],
                                       4095.0 - W2 * (p - 1), None, ALU.add))
            dve.tensor_scalar(less_rel[:], rel[:], -1.0, None, ALU.mult)
            link(dve.tensor_scalar(less_src[:], srcf[:], -1.0, None, ALU.mult))
            dve.sem_inc(tables, 1)
            dve.wait_ge(zeroed, 1)
            dve.wait_ge(far_in, 33)
            link(dve.tensor_reduce(far_max[:], far_row[:], AX, ALU.max))
            link(dve.tensor_copy(far_flag[:], far_max[:]))
            dve.sem_inc(flag_ready, 1)
            dve.sem_inc(bank_free, NCH)
            dve.sem_inc(bank2_free, NCH)
            dve.sem_inc(unit_done, 1)
            dve.sem_inc(unit2_done, 1)
            dve.sem_inc(carried, 1)

            def make(p, g, b):
                wait_used(dve, p * G + g)
                for k in range(DVE_K):
                    last = one_hot(p, g, b, k)
                last.then_inc(oh_v, 1)

            def add_up(p, g):
                n = p * G + g
                at = dve.value_load(group_reg[0:1, 0, bass.ds(n, 1)], min_val=0, max_val=T - 2)
                pair, before = second(dve, n)

                def add(w, done, free, u0):
                    dve.wait_ge(free, u0 + NCH)
                    for j, (c0, cn) in enumerate(CH):
                        dve.wait_ge(done, u0 + j + 1 + 1)
                        a = Af[:, bass.ds(at + w, 1), c0:c0 + cn].rearrange("p a n -> p (a n)")
                        dve.tensor_tensor(a, a, acc[:, w * NCH + j, 0:cn], ALU.add).then_inc(free, 1)

                dve.wait_ge(bank2_free, before * NCH + NCH)
                add(0, unit_done, bank_free, n * NCH)
                with dve.If(pair > 0):
                    dve.wait_ge(bank_free, n * NCH + 2 * NCH)
                    add(1, unit2_done, bank2_free, before * NCH)

            def one_pass(p):
                if isinstance(p, int):
                    for k in range(DVE_K):
                        last = one_hot(p, 0, 0, k)
                    last.then_inc(oh_v, 1)
                else:
                    dve.wait_ge(oh_v, p * (G + 1))
                    make(p, 0, 0)
                with dve.Fori(0, G // 2) as pair:
                    g = pair * 2
                    make(p, g + 1, 1)
                    add_up(p, g)
                    make(p, g + 2, 0)
                    add_up(p, g + 1)

            one_pass(0)
            flag = dve.value_load(far_flag[0:1, 0:1], min_val=0, max_val=1)
            with dve.If(flag > 0):
                with dve.Fori(1, PASSES) as p:
                    one_pass(p)
            dve.drain()
            dve.tensor_copy(A[:, 0:T // 2], Af[:, 0:T // 2]).then_inc(a_bf, 1)
            dve.tensor_copy(A[:, T // 2:], Af[:, T // 2:]).then_inc(a_bf, 1)
            for u in range(1, 2 * T, 2):
                dve.wait_ge(tr_done, u + 1)
                dve.tensor_copy(turned_to(u), tr[:, u % 2, 0:5, 0:R]).then_inc(tr_free[1], 1)
            dve.wait_ge(tr_free[1], T)

        @block.gpsimd
        def _(pool):
            pool.iota(iota_i[:], pattern=[[1, N]], base=0, channel_multiplier=0).then_inc(iotas, 1)
            pool.iota(steps_i[:], pattern=[[R, 8]], base=R, channel_multiplier=0).then_inc(iotas, 1)
            pool.memset(Af[:], 0.0).then_inc(zeroed, 1)

            def make(p, g, b, first=False):
                if not first:
                    wait_used(pool, p * G + g)
                pool.tensor_copy(now_dst[:, b, :], rel[:, bass.ds(p * (G * EG) + g * EG + DVE_K, POOL_K)])
                pool.tensor_copy(now_src[:, b, :], srcf[:, bass.ds(g * EG + DVE_K, POOL_K)]).then_inc(now, 1)
                pool.wait_ge(now, p * (G + 1) + g + 1)
                carry_wait(pool, c, carried, p * (G + 1) + g + 1)
                for k in range(DVE_K, DVE_K + POOL_K):
                    n = k - DVE_K
                    pool.tensor_scalar(oh_dst[:, b, k, :], iota[:, 0:W2], now_dst[:, b, n:n + 1], None, ALU.is_equal)
                    last = pool.tensor_scalar(oh_src[:, b, k, :], iota[:], now_src[:, b, n:n + 1], None, ALU.is_equal)
                last.then_inc(oh_p, 1)

            def one_pass(p):
                if not isinstance(p, int):
                    pool.wait_ge(oh_p, p * (G + 1))
                make(p, 0, 0, first=isinstance(p, int))
                with pool.Fori(0, G // 2) as pair:
                    g = pair * 2
                    make(p, g + 1, 1)
                    make(p, g + 2, 0)

            pool.wait_ge(tables, 1)
            one_pass(0)
            pool.wait_ge(flag_ready, 1)
            flag = pool.value_load(far_flag[0:1, 0:1], min_val=0, max_val=1)
            with pool.If(flag > 0):
                with pool.Fori(1, PASSES) as p:
                    one_pass(p)

        @block.tensor
        def _(pe):
            def products(p, g, b):
                pe.wait_ge(oh_v, p * (G + 1) + g + 1)
                pe.wait_ge(oh_p, p * (G + 1) + g + 1)
                pe.wait_ge(oh_a, p * (G + 1) + g + 1)
                n = p * G + g
                pair, before = second(pe, n)

                def window(w, done, free, u0):
                    for j, (c0, cn) in enumerate(CH):
                        pe.wait_ge(free, u0 + j + 1)
                        for k in range(EG):
                            mm = pe.matmul(acc[:, w * NCH + j, 0:cn], oh_dst[:, b, k, w * R:(w + 1) * R],
                                           oh_src[:, b, k, c0:c0 + cn], start=(k == 0), stop=(k == EG - 1))
                        mm.then_inc(done, 1)

                window(0, unit_done, bank_free, n * NCH)
                with pe.If(pair > 0):
                    window(1, unit2_done, bank2_free, before * NCH)

            def one_pass(p):
                with pe.Fori(0, G // 2) as pair:
                    g = pair * 2
                    products(p, g, 0)
                    products(p, g + 1, 1)

            pe.wait_ge(tables, 1)
            one_pass(0)
            pe.wait_ge(flag_ready, 1)
            flag = pe.value_load(far_flag[0:1, 0:1], min_val=0, max_val=1)
            with pe.If(flag > 0):
                with pe.Fori(1, PASSES) as p:
                    one_pass(p)
            for u in range(2 * T):
                half, st = u // T, u % T
                if st == 0:
                    pe.wait_ge(a_bf, half + 1)
                if u >= 2:
                    pe.wait_ge(tr_free[u % 2], u // 2)
                for j in range(5):
                    t = pe.transpose(tr[:, u % 2, j, 0:R], A[:, half * 5 + j, st * R:(st + 1) * R],
                                     c["ident16"][0:R, 0:R])
                t.then_inc(tr_done, 1)

        @block.scalar
        def _(act):
            act.wait_ge(tables, 1)

            def make(p, g, b, first=False):
                if not first:
                    wait_used(act, p * G + g)
                e = p * (G * EG) + g * EG + ACT_K
                act.activation(gap[:, 0:W2], iota[:, 0:W2], ACT.Abs, bias=less_rel[:, bass.ds(e, 1)])
                act.activation(gap[:, W2:], iota[:], ACT.Abs, bias=less_src[:, bass.ds(g * EG + ACT_K, 1)]).then_inc(gaps, 1)
                act.wait_ge(gaps, p * (G + 1) + g + 1)
                act.activation(oh_dst[:, b, ACT_K, :], gap[:, 0:W2], ACT.Relu, scale=-1.0, bias=1.0)
                act.activation(oh_src[:, b, ACT_K, :], gap[:, W2:], ACT.Relu, scale=-1.0, bias=1.0).then_inc(oh_a, 1)
                act.wait_ge(oh_a, p * (G + 1) + g + 1)

            def one_pass(p):
                make(p, 0, 0, first=isinstance(p, int))
                with act.Fori(0, G // 2) as pair:
                    g = pair * 2
                    make(p, g + 1, 1)
                    make(p, g + 2, 0)

            one_pass(0)
            act.wait_ge(flag_ready, 1)
            flag = act.value_load(far_flag[0:1, 0:1], min_val=0, max_val=1)
            with act.If(flag > 0):
                with act.Fori(1, PASSES) as p:
                    one_pass(p)
            for u in range(0, 2 * T, 2):
                act.wait_ge(tr_done, u + 1)
                act.activation(turned_to(u), tr[:, u % 2, 0:5, 0:R], ACT.Copy).then_inc(tr_free[0], 1)
            act.wait_ge(tr_free[0], T)


def products3(pe, out, w, x, first, last):
    (wh, wl), (xh, xl) = w, x
    pe.matmul(out, wh, xh, start=first, stop=False)
    pe.matmul(out, wh, xl, start=False, stop=False)
    return pe.matmul(out, wl, xh, start=False, stop=last)


def rows(t, n=R):
    return slice(t * n, (t + 1) * n)


def row_moments(dve, link, x, stats, mv, arrival=lambda t: None):
    for t in range(T):
        arrival(t)
        d = dve.bn_stats(stats[:, t, :], x[:, t, :])
    link(d)
    for t in range(T):
        d = dve.bn_aggr(mv[:, t, :], stats[:, t, :])
    link(d)


def inverse_root(dve, link, y, v, r, factor=1.0):
    link(dve.reciprocal(y, r))
    link(dve.tensor_tensor(r, y, y, ALU.mult))
    link(dve.tensor_tensor(r, r, v, ALU.mult))
    link(dve.tensor_scalar(r, r, -0.5 * factor, 1.5 * factor, ALU.mult, ALU.add))
    link(dve.tensor_tensor(y, y, r, ALU.mult))


def stage_pre(nc, c, x, w_init_t, w_qkv, norm_w, h_dram, fm, wq, rn):
    with Stage(nc, "pre") as s:
        xs = s.sb("x", [R, T, D])
        wi_raw = s.sb("wi_raw", [128, K, D])
        wi = s.sb("wi", [128, 2, K, D], F32R)
        wq_raw = s.sb("wq_raw", [128, K, 3 * D])
        nw = s.sb("nw", [128, K])
        stats = s.sb("stats", [R, T, 6])
        mv = s.sb("mv", [R, T, 2])
        rstd = s.sb("rstd", [R, T])
        var = s.sb("var", [R, T])
        root = s.sb("root", [R, T])
        sq = s.sb("sq", [R, D])
        ss = s.sb("ss", [R, T])
        h = s.sb("h", [R, 2, D])
        h3 = s.sb("h3", [R, 2, 3, D], BF16)
        rest = s.sb("rest", [R, 2, D])
        tp = s.ps("tp", [128, 2, K, 128])
        hp = s.ps("hp", [R, 2, D])
        x_in = [s.sem(f"x_in{j}") for j in range(T // 2)]
        w_in = s.sem("w_in")
        chain = s.sem("chain")
        moments = s.sem("moments")
        rooted = s.sem("rooted")
        xn_ready = s.sem("xn_ready")
        squares = s.sem("squares")
        turned = s.sem("turned")
        fm_hi = s.sem("fm_hi")
        fm_ready = s.sem("fm_ready")
        wi_hi = s.sem("wi_hi")
        wi_ready = s.sem("wi_ready")
        h_done = s.sem("h_done")
        h_up = s.sem("h_up")
        h_split = s.sem("h_split")
        h_out = [s.sem(f"h_out{b}") for b in range(2)]
        wq_scaled = s.sem("wq_scaled")
        wq_hi = s.sem("wq_hi")
        block = s.block()

        @block.sync
        def _(sp):
            for j in range(T // 2):
                sp.dma_start(xs[:, 2 * j:2 * j + 2], x[rows(j, 2 * R), :].rearrange("(t p) d -> p t d", p=R))\
                  .then_inc(x_in[j], 16)
            sp.dma_start(wi_raw[:], w_init_t.rearrange("(k p) n -> p k n", p=128)).then_inc(w_in, 16)
            sp.dma_start(nw[:], norm_w).then_inc(w_in, 16)
            sp.dma_start(wq_raw[:], w_qkv.rearrange("(k p) n -> p k n", p=128)).then_inc(w_in, 16)
            for t in range(T):
                sp.wait_ge(h_split, 3 * (t + 1))
                sp.dma_start(h_dram[rows(t), :, :], h3[:, t % 2]).then_inc(h_out[t % 2], 16)
            for b in range(2):
                sp.wait_ge(h_out[b], 16 * T // 2)

        @block.vector
        def _(dve):
            link = Chain(dve, chain)

            def norm(t):
                dve.tensor_scalar(xs[:, t, :], xs[:, t, :], mv[:, t, 0:1], rstd[:, t:t + 1],
                                  ALU.subtract, ALU.mult).then_inc(xn_ready, 1)

            def low_part(t):
                dve.wait_ge(fm_hi, t + 1)
                dve.tensor_tensor(fm[:, 1, :, rows(t)], tp[:, t % 2, :, 0:R],
                                  fm[:, 0, :, rows(t)].bitcast(F32), ALU.subtract).then_inc(fm_ready, 1)

            def split_h(t):
                b = t % 2
                dve.wait_ge(h_up, t + 1)
                if t >= 2:
                    dve.wait_ge(h_out[b], 16 * (t // 2))
                link(dve.tensor_copy(h3[:, b, 0, :], h[:, b, :]))
                dve.sem_inc(h_split, 1)
                link(dve.tensor_tensor(rest[:, b, :], h[:, b, :], h3[:, b, 0, :], ALU.subtract))
                link(dve.tensor_copy(h3[:, b, 1, :], rest[:, b, :]))
                dve.sem_inc(h_split, 1)
                dve.tensor_tensor(h3[:, b, 2, :], rest[:, b, :], h3[:, b, 1, :], ALU.subtract).then_inc(h_split, 1)

            row_moments(dve, link, xs, stats, mv, lambda t: dve.wait_ge(x_in[t // 2], 16))
            link(dve.tensor_scalar(var[:], mv[:, :, 1], 1e-5, None, ALU.add))
            dve.sem_inc(moments, 1)
            dve.wait_ge(rooted, 1)
            inverse_root(dve, link, rstd[:], var[:], root[:])
            norm(0)
            norm(1)
            dve.wait_ge(wi_hi, 1)
            dve.tensor_tensor(wi[:, 1], wi_raw[:], wi[:, 0].bitcast(F32), ALU.subtract).then_inc(wi_ready, 1)
            for t in range(T):
                low_part(t)
                if t + 2 < T:
                    norm(t + 2)
                if t >= 1:
                    split_h(t - 1)
            split_h(T - 1)
            dve.wait_ge(squares, T)
            link(dve.tensor_scalar(ss[:], ss[:], 1e-24, None, ALU.max))
            dve.sem_inc(moments, 1)
            dve.wait_ge(rooted, 2)
            inverse_root(dve, link, rn[:], ss[:], root[:], float(D) ** 0.5)
            for k in range(K):
                dve.wait_ge(wq_hi, k + 1)
                dve.tensor_tensor(wq[:, 1, k, :], wq_raw[:, k, :], wq[:, 0, k, :].bitcast(F32), ALU.subtract)
            dve.drain()

        @block.gpsimd
        def _(pool):
            pool.wait_ge(w_in, 48)
            for k in range(K):
                pool.tensor_scalar(wq_raw[:, k, :], wq_raw[:, k, :], nw[:, k:k + 1], None, ALU.mult)\
                    .then_inc(wq_scaled, 1)
                pool.wait_ge(wq_scaled, k + 1)
                pool.tensor_copy(wq[:, 0, k, :], wq_raw[:, k, :]).then_inc(wq_hi, 1)

        @block.tensor
        def _(pe):
            def turn(t):
                pe.wait_ge(xn_ready, t + 1)
                if t >= 2:
                    pe.wait_ge(fm_ready, t - 1)
                for k in range(K):
                    p = pe.transpose(tp[:, t % 2, k, 0:R], xs[:, t, k * 128:(k + 1) * 128], c["ident"][0:R, 0:R])
                p.then_inc(turned, 1)

            def first_layer(t):
                pe.wait_ge(fm_ready, t + 1)
                if t >= 2:
                    pe.wait_ge(h_up, t - 1)
                for k in range(K):
                    p = products3(pe, hp[:, t % 2, :], (fm[:, 0, k, rows(t)], fm[:, 1, k, rows(t)]),
                                  (wi[:, 0, k, :], wi[:, 1, k, :]), k == 0, k == K - 1)
                p.then_inc(h_done, 1)

            turn(0)
            turn(1)
            pe.wait_ge(wi_ready, 1)
            for t in range(T):
                first_layer(t)
                if t + 2 < T:
                    turn(t + 2)

        @block.scalar
        def _(act):
            act.wait_ge(w_in, 48)
            act.activation(wi[:, 0], wi_raw[:], ACT.Copy).then_inc(wi_hi, 1)
            act.wait_ge(moments, 1)
            act.activation(root[:], var[:], ACT.Sqrt).then_inc(rooted, 1)

            def high_part(t):
                act.wait_ge(turned, t + 1)
                act.activation(fm[:, 0, :, rows(t)], tp[:, t % 2, :, 0:R], ACT.Copy).then_inc(fm_hi, 1)

            def up(t):
                act.wait_ge(h_done, t + 1)
                if t >= 2:
                    act.wait_ge(h_split, 3 * (t - 1))
                act.activation(h[:, t % 2, :], hp[:, t % 2, :], ACT.Relu).then_inc(h_up, 1)

            high_part(0)
            for t in range(T):
                if t >= 1:
                    act.wait_ge(squares, t)
                act.activation(sq[:], xs[:, t, :], ACT.Square, accum_out=ss[:, t:t + 1]).then_inc(squares, 1)
                if t + 1 < T:
                    high_part(t + 1)
                up(t)
            act.wait_ge(moments, 2)
            act.activation(root[:], ss[:], ACT.Sqrt).then_inc(rooted, 1)


def stage_qkv(nc, c, fm, wq, rn, q, k_, v2):
    with Stage(nc, "qkv") as s:
        acc = s.ps("acc", [R, 8, D])
        done = s.sem("done")
        by_act = s.sem("by_act")
        by_dve = s.sem("by_dve")
        block = s.block()

        @block.tensor
        def _(pe):
            for u in range(3 * T):
                t, j = u // 3, u % 3
                if u >= 8:
                    t0, j0 = (u - 8) // 3, (u - 8) % 3
                    pe.wait_ge((by_act, by_dve, by_dve)[j0], 2 * t0 + (1, 1, 2)[j0])
                for k in range(K):
                    p = products3(pe, acc[:, u % 8, :], (fm[:, 0, k, rows(t)], fm[:, 1, k, rows(t)]),
                                  (wq[:, 0, k, rows(j, D)], wq[:, 1, k, rows(j, D)]), k == 0, k == K - 1)
                p.then_inc(done, 1)

        @block.scalar
        def _(act):
            for t in range(T):
                act.wait_ge(done, 3 * t + 1)
                act.activation(q[:, t, :], acc[:, (3 * t) % 8, :], ACT.Copy, scale=rn[:, t:t + 1]).then_inc(by_act, 1)
                act.wait_ge(done, 3 * t + 3)
                act.activation(v2[:, 0, t, :], acc[:, (3 * t + 2) % 8, :], ACT.Copy, scale=rn[:, t:t + 1])\
                   .then_inc(by_act, 1)
            act.wait_ge(by_act, 2 * T)

        @block.vector
        def _(dve):
            for t in range(T):
                dve.wait_ge(done, 3 * t + 2)
                dve.tensor_scalar(k_[:, t, :], acc[:, (3 * t + 1) % 8, :], rn[:, t:t + 1], None, ALU.mult)\
                   .then_inc(by_dve, 1)
                dve.wait_ge(by_act, 2 * t + 2)
                dve.scalar_tensor_tensor(out=v2[:, 1, t, :], in0=acc[:, (3 * t + 2) % 8, :], scalar=rn[:, t:t + 1],
                                         in1=v2[:, 0, t, :].bitcast(F32), op0=ALU.mult, op1=ALU.subtract)\
                   .then_inc(by_dve, 1)
            dve.wait_ge(by_dve, 2 * T)


def stage_mix(nc, c, x, q, k_, v2, mem_fm, mem_rows, w_out, b_out, out_norm_w, out):
    H, C, NM = 8, 64, 8
    with Stage(nc, "mix") as s:
        kmax = s.sb("kmax", [R, D])
        kmx = s.sb("kmx", [128, K])
        mmx = s.sb("mmx", [128, K])
        diag = s.sb("diag", [128, K, 128])
        kmb = s.sb("kmb", [R, D])
        mem = s.sb("mem", [128, K, NM])
        eighth = s.sb("eighth", [R, 1])
        mk = s.sb("mk", [NM, D])
        mv_ = s.sb("mv", [NM, D])
        mk2 = s.sb("mk2", [NM, 2, D], F32R)
        mv2 = s.sb("mv2", [NM, 2, D], F32R)
        ek = s.sb("ek", [R, 2, T, D], F32R)
        ones2 = s.sb("ones2", [R, 2], F32R)
        den = s.sb("den", [128, K])
        ctx = s.sb("ctx", [128, 2, K, 128], F32R)
        wo_raw = s.sb("wo_raw", [128, K, D])
        wo = s.sb("wo", [128, 2, K, D], F32R)
        m = s.sb("m", [128, 2, K, D], F32R)
        ms = s.sb("ms", [128, D])
        qm = s.sb("qm", [R, 2, H])
        qs = s.sb("qs", [R, 2, H])
        q2 = s.sb("q2", [128, 2, 2, K, R], F32R)
        o = s.sb("o", [R, 2, D])
        xin = s.sb("xin", [R, 2, D])
        sq = kmax
        kc = o
        mkc = kmax[0:NM, :]
        ss = s.sb("ss", [R, T])
        sr = s.sb("sr", [R, T])
        rt = s.sb("rt", [R, T])
        bo = s.sb("bo", [R, D])
        nw = s.sb("nw", [R, D])
        kt = s.ps("kt", [128, K, 128])
        kb = s.ps("kb", [R, D])
        cp = s.ps("cp", [128, K, 128])
        dp = s.ps("dp", [128, K, 2])
        mo = s.ps("mo", [128, 2, D])
        qt = s.ps("qt", [128, 2, K, 128])

        loaded = s.sem("loaded")
        chain = s.sem("chain")
        kmax_ready = s.sem("kmax_ready")
        kmax_turned = s.sem("kmax_turned")
        diag_ready = s.sem("diag_ready")
        kmb_done = s.sem("kmb_done")
        k_less = s.sem("k_less")
        k_made = s.sem("k_made")
        mem_made = s.sem("mem_made")
        k_exp = s.sem("k_exp")
        ek_hi = s.sem("ek_hi")
        ek_ready = s.sem("ek_ready")
        mem_less = s.sem("mem_less")
        mem_exp = s.sem("mem_exp")
        mem_ready = s.sem("mem_ready")
        wo_hi = s.sem("wo_hi")
        ctx_done = s.sem("ctx_done")
        ctx_hi = s.sem("ctx_hi")
        ctx_ready = s.sem("ctx_ready")
        m_done = s.sem("m_done")
        m_scaled = s.sem("m_scaled")
        m_hi = s.sem("m_hi")
        m_ready = s.sem("m_ready")
        q_less = s.sem("q_less")
        q_exp = s.sem("q_exp")
        q_ready = s.sem("q_ready")
        q_turned = s.sem("q_turned")
        q_hi = s.sem("q_hi")
        q_lo = s.sem("q_lo")
        o_done = s.sem("o_done")
        o_biased = s.sem("o_biased")
        o_sq = s.sem("o_sq")
        o_ready = s.sem("o_ready")
        x_in = [s.sem(f"x_in{b}") for b in range(2)]
        stored = [s.sem(f"stored{b}") for b in range(2)]
        o_root = s.sem("o_root")
        o_clamped = s.sem("o_clamped")
        ones_ready = s.sem("ones_ready")
        block = s.block()
        heads = lambda ap: ap.rearrange("p (h c) -> p h c", h=H)

        @block.sync
        def _(sp):
            sp.dma_start(mem[:], mem_fm.rearrange("(k p) m -> p k m", p=128)).then_inc(loaded, 16)
            sp.dma_start(mk[:], mem_rows[0]).then_inc(loaded, 16)
            sp.dma_start(mv_[:], mem_rows[1]).then_inc(loaded, 16)
            sp.dma_start(wo_raw[:], w_out.rearrange("(k p) n -> p k n", p=128)).then_inc(loaded, 16)
            sp.dma_start(bo[:], b_out.partition_broadcast(R)).then_inc(loaded, 16)
            sp.dma_start(nw[:], out_norm_w.partition_broadcast(R)).then_inc(loaded, 16)
            for t in range(T + 1):
                if t < T:
                    if t >= 2:
                        sp.wait_ge(o_ready, t - 1)
                    sp.dma_start(xin[:, t % 2, :], x[rows(t), :]).then_inc(x_in[t % 2], 16)
                if t >= 1:
                    sp.wait_ge(o_ready, t)
                    sp.dma_start(out[rows(t - 1), :], o[:, (t - 1) % 2, :])\
                      .then_inc(stored[(t - 1) % 2], 16)
            for b in range(2):
                sp.wait_ge(stored[b], 16 * T // 2)

        @block.vector
        def _(dve):
            link = Chain(dve, chain)
            dve.memset(ctx[:].bitcast(F32), 0.0)
            link(dve.tensor_copy(kmax[:], k_[:, 0, :]))
            for t in range(1, T):
                link(dve.tensor_tensor(kmax[:], kmax[:], k_[:, t, :], ALU.max))
            dve.sem_inc(kmax_ready, 1)
            dve.wait_ge(kmax_turned, 1)
            link(dve.tensor_reduce(kmx[:], kt[:, :, 0:R], AX, ALU.max))
            dve.wait_ge(loaded, 96)
            link(dve.tensor_reduce(mmx[:], mem[:], AX, ALU.max))
            link(dve.tensor_tensor(kmx[:], kmx[:], mmx[:], ALU.max))
            for j in range(K):
                d = dve.tensor_scalar(diag[:, j, :], c["ident"][:], kmx[:, j:j + 1], None, ALU.mult)
            d.then_inc(diag_ready, 1)
            dve.wait_ge(kmb_done, 1)
            link(dve.tensor_copy(kmb[:], kb[:]))
            NEAREST_4TH = 1.5 * 2 ** 21

            def cut(a, cc):
                link(dve.tensor_scalar(cc, a, NEAREST_4TH, NEAREST_4TH, ALU.add, ALU.subtract))
                return dve.tensor_tensor(a, a, cc, ALU.subtract)

            def join(a, cc):
                return dve.scalar_tensor_tensor(out=a, in0=a, scalar=2.0, in1=cc, op0=ALU.min, op1=ALU.mult)

            link(dve.memset(eighth[:], -0.125))
            link(dve.tensor_tensor(mk[:], mk[:], kmb[0:NM, :], ALU.subtract))
            cut(mk[:], mkc).then_inc(mem_less, 1)

            def k_cut(t):
                link(dve.tensor_tensor(k_[:, t, :], k_[:, t, :], kmb[:], ALU.subtract))
                cut(k_[:, t, :], kc[:, t % 2, :]).then_inc(k_less, 1)

            def k_join(t):
                dve.wait_ge(k_exp, t + 1)
                join(k_[:, t, :], kc[:, t % 2, :]).then_inc(k_made, 1)
                dve.wait_ge(k_made, t + 1)

            def q_cut(t):
                link(dve.tensor_reduce(qm[:, t % 2, :], heads(q[:, t, :]), AX, ALU.max))
                link(dve.tensor_tensor(heads(q[:, t, :]), heads(q[:, t, :]),
                                       qm[:, t % 2, :].unsqueeze(2).to_broadcast([R, H, C]), ALU.subtract))
                cut(q[:, t, :], kc[:, t % 2, :]).then_inc(q_less, 1)

            def q_norm(t):
                dve.wait_ge(q_exp, t + 1)
                link(join(q[:, t, :], kc[:, t % 2, :]))
                link(dve.tensor_reduce(qs[:, t % 2, :], heads(q[:, t, :]), AX, ALU.add))
                link(dve.reciprocal(qs[:, t % 2, :], qs[:, t % 2, :]))
                link(dve.tensor_scalar(qs[:, t % 2, :], qs[:, t % 2, :], float(C) ** -0.5, None, ALU.mult))
                dve.tensor_tensor(heads(q[:, t, :]), heads(q[:, t, :]),
                                  qs[:, t % 2, :].unsqueeze(2).to_broadcast([R, H, C]), ALU.mult)\
                   .then_inc(q_ready, 1)

            def ek_low(t):
                dve.wait_ge(ek_hi, t + 1)
                dve.tensor_tensor(ek[:, 1, t, :], k_[:, t, :], ek[:, 0, t, :].bitcast(F32), ALU.subtract)\
                   .then_inc(ek_ready, 1)

            k_cut(0)
            dve.wait_ge(mem_exp, 1)
            join(mk[:], mkc).then_inc(mem_made, 1)
            for t in range(T):
                if t + 1 < T:
                    k_cut(t + 1)
                k_join(t)
                if t >= 1:
                    ek_low(t - 1)
            ek_low(T - 1)
            q_cut(0)
            for t in range(T):
                if t + 1 < T:
                    q_cut(t + 1)
                q_norm(t)
            dve.wait_ge(wo_hi, 1)
            dve.tensor_tensor(wo[:, 1], wo_raw[:], wo[:, 0].bitcast(F32), ALU.subtract).then_inc(ctx_ready, 1)
            dve.wait_ge(ctx_hi, 1)
            for h in range(2):
                d = dve.tensor_tensor(ctx[64 * h:64 * h + 64, 1, :, 64 * h:64 * h + 64],
                                      cp[64 * h:64 * h + 64, :, 64 * h:64 * h + 64],
                                      ctx[64 * h:64 * h + 64, 0, :, 64 * h:64 * h + 64].bitcast(F32), ALU.subtract)
            d.then_inc(ctx_ready, 1)
            link(dve.reciprocal(den[:], dp[:, :, 0]))
            for j in range(K):
                dve.wait_ge(m_done, j + 1)
                if j:
                    dve.wait_ge(m_ready, j)
                dve.tensor_scalar(ms[:], mo[:, j % 2, :], den[:, j:j + 1], None, ALU.mult).then_inc(m_scaled, 1)
                dve.wait_ge(m_hi, j + 1)
                dve.tensor_tensor(m[:, 1, j, :], ms[:], m[:, 0, j, :].bitcast(F32), ALU.subtract).then_inc(m_ready, 1)

            def q_low(t):
                dve.wait_ge(q_hi, t + 1)
                dve.tensor_tensor(q2[:, t % 2, 1], qt[:, t % 2, :, 0:R], q2[:, t % 2, 0].bitcast(F32), ALU.subtract)\
                   .then_inc(q_lo, 1)

            q_low(0)
            for t in range(T):
                b = t % 2
                if t + 1 < T:
                    q_low(t + 1)
                dve.wait_ge(o_done, t + 1)
                if t >= 2:
                    dve.wait_ge(stored[b], 16 * (t // 2))
                dve.tensor_tensor(o[:, b, :], mo[0:R, b, :], bo[:], ALU.add).then_inc(o_biased, 1)
                dve.wait_ge(o_sq, t + 1)
                dve.tensor_scalar(ss[:, t:t + 1], ss[:, t:t + 1], 1e-24, None, ALU.max).then_inc(o_clamped, 1)
                dve.wait_ge(o_root, t + 1)
                inverse_root(dve, link, rt[:, t:t + 1], ss[:, t:t + 1], sr[:, t:t + 1], float(D) ** 0.5)
                link(dve.scalar_tensor_tensor(out=o[:, b, :], in0=o[:, b, :], scalar=rt[:, t:t + 1], in1=nw[:],
                                              op0=ALU.mult, op1=ALU.mult))
                dve.wait_ge(x_in[b], 16 * (t // 2 + 1))
                dve.tensor_tensor(o[:, b, :], o[:, b, :], xin[:, b, :], ALU.add).then_inc(o_ready, 1)

        @block.gpsimd
        def _(pool):
            pool.memset(ones2[:].bitcast(F32), 1.0).then_inc(ones_ready, 1)
            pool.wait_ge(loaded, 96)
            pool.tensor_copy(wo[:, 0], wo_raw[:]).then_inc(wo_hi, 1)
            pool.tensor_copy(mv2[:, 0, :], mv_[:]).then_inc(mem_ready, 1)
            pool.wait_ge(mem_ready, 1)
            pool.tensor_tensor(mv2[:, 1, :], mv_[:], mv2[:, 0, :].bitcast(F32), ALU.subtract).then_inc(mem_ready, 1)
            pool.wait_ge(mem_made, 1)
            pool.tensor_copy(mk2[:, 0, :], mk[:]).then_inc(mem_ready, 1)
            pool.wait_ge(mem_ready, 3)
            pool.tensor_tensor(mk2[:, 1, :], mk[:], mk2[:, 0, :].bitcast(F32), ALU.subtract).then_inc(mem_ready, 1)
            for t in range(T):
                pool.wait_ge(k_made, t + 1)
                pool.tensor_copy(ek[:, 0, t, :], k_[:, t, :]).then_inc(ek_hi, 1)
            for j in range(K):
                pool.wait_ge(m_scaled, j + 1)
                pool.tensor_copy(m[:, 0, j, :], ms[:]).then_inc(m_hi, 1)
            pool.wait_ge(m_hi, K)

        @block.scalar
        def _(act):
            act.wait_ge(mem_less, 1)
            act.activation(mkc, mkc, ACT.Exp, bias=eighth[0:NM, :])
            act.activation(mk[:], mk[:], ACT.Exp).then_inc(mem_exp, 1)
            for t in range(T):
                act.wait_ge(k_less, t + 1)
                act.activation(kc[:, t % 2, :], kc[:, t % 2, :], ACT.Exp, bias=eighth[:])
                act.activation(k_[:, t, :], k_[:, t, :], ACT.Exp).then_inc(k_exp, 1)
            for t in range(T):
                act.wait_ge(q_less, t + 1)
                act.activation(kc[:, t % 2, :], kc[:, t % 2, :], ACT.Exp, bias=eighth[:])
                act.activation(q[:, t, :], q[:, t, :], ACT.Exp).then_inc(q_exp, 1)
            act.wait_ge(ctx_done, 1)
            for h in range(2):
                a = act.activation(ctx[64 * h:64 * h + 64, 0, :, 64 * h:64 * h + 64],
                                   cp[64 * h:64 * h + 64, :, 64 * h:64 * h + 64], ACT.Copy)
            a.then_inc(ctx_hi, 1)

            def q_high(t):
                act.wait_ge(q_turned, t + 1)
                if t >= 2:
                    act.wait_ge(o_done, t - 1)
                act.activation(q2[:, t % 2, 0], qt[:, t % 2, :, 0:R], ACT.Copy).then_inc(q_hi, 1)

            q_high(0)
            for t in range(T):
                if t + 1 < T:
                    q_high(t + 1)
                act.wait_ge(o_biased, t + 1)
                act.activation(sq[:], o[:, t % 2, :], ACT.Square, accum_out=ss[:, t:t + 1]).then_inc(o_sq, 1)
                act.wait_ge(o_clamped, t + 1)
                act.activation(sr[:, t:t + 1], ss[:, t:t + 1], ACT.Sqrt).then_inc(o_root, 1)
            act.wait_ge(o_root, T)

        @block.tensor
        def _(pe):
            pe.wait_ge(kmax_ready, 1)
            for j in range(K):
                p = pe.transpose(kt[:, j, 0:R], kmax[:, rows(j, 128)], c["ident"][0:R, 0:R])
            p.then_inc(kmax_turned, 1)
            pe.wait_ge(diag_ready, 1)
            for j in range(K):
                p = pe.matmul(kb[:, rows(j, 128)], c["ones"][:, 0:R], diag[:, j, :], start=True, stop=True)
            p.then_inc(kmb_done, 1)
            pe.wait_ge(ones_ready, 1)
            pe.wait_ge(mem_ready, 4)
            pe.wait_ge(ek_ready, T)
            for j in range(K):
                cols = rows(j, 128)
                for t in range(T):
                    products3(pe, cp[:, j, :], (v2[:, 0, t, cols], v2[:, 1, t, cols]),
                              (ek[:, 0, t, cols], ek[:, 1, t, cols]), t == 0, False)
                products3(pe, cp[:, j, :], (mv2[:, 0, cols], mv2[:, 1, cols]),
                          (mk2[:, 0, cols], mk2[:, 1, cols]), False, True)
            for j in range(K):
                cols = rows(j, 128)
                for t in range(T):
                    for part in range(2):
                        pe.matmul(dp[:, j, :], ek[:, part, t, cols], ones2[:], start=(t == 0 and part == 0), stop=False)
                pe.matmul(dp[:, j, :], mk2[:, 0, cols], ones2[0:NM, :], start=False, stop=False)
                p = pe.matmul(dp[:, j, :], mk2[:, 1, cols], ones2[0:NM, :], start=False, stop=True)
            p.then_inc(ctx_done, 1)
            pe.wait_ge(ctx_ready, 2)
            for j in range(K):
                if j >= 2:
                    pe.wait_ge(m_scaled, j - 1)
                products3(pe, mo[:, j % 2, :], (ctx[:, 0, j, :], ctx[:, 1, j, :]),
                          (wo[:, 0, j, :], wo[:, 1, j, :]), True, True).then_inc(m_done, 1)

            def turn(t):
                pe.wait_ge(q_ready, t + 1)
                if t >= 2:
                    pe.wait_ge(q_lo, t - 1)
                for j in range(K):
                    p = pe.transpose(qt[:, t % 2, j, 0:R], q[:, t, rows(j, 128)], c["ident"][0:R, 0:R])
                p.then_inc(q_turned, 1)

            turn(0)
            pe.wait_ge(m_ready, K)
            for t in range(T):
                b = t % 2
                if t + 1 < T:
                    turn(t + 1)
                pe.wait_ge(q_lo, t + 1)
                if t >= 2:
                    pe.wait_ge(o_biased, t - 1)
                for j in range(K):
                    p = products3(pe, mo[0:R, b, :], (q2[:, b, 0, j, :], q2[:, b, 1, j, :]),
                                  (m[:, 0, j, :], m[:, 1, j, :]), j == 0, j == K - 1)
                p.then_inc(o_done, 1)


LAYERS = 3
KC = 3 * K


def stage_fuse(nc, c, w_fwd, w_bwd, w_self_t, wc_dram):
    with Stage(nc, "fuse") as s:
        wx_raw = s.sb("wx_raw", [128, 2, 2, K, D])
        wx = s.sb("wx", [128, 2, 2, K, D], F32R)
        ws_raw = s.sb("ws_raw", [128, 2, KC, D])
        ws = s.sb("ws", [128, 2, KC, D], F32R)
        wo = s.sb("wo", [128, 2, 2, D], F32R)
        acc = s.ps("acc", [128, 4, D])
        raw_in = [[s.sem(f"raw_in{b}{i}") for i in range(3)] for b in range(2)]
        hi_x = s.sem("hi_x")
        hi_s = s.sem("hi_s")
        hi_self = s.sem("hi_self")
        lo = s.sem("lo")
        done = s.sem("done")
        hi_o = s.sem("hi_o")
        lo_o = s.sem("lo_o")
        self_out = s.sem("self_out")
        out = [s.sem(f"out{b}") for b in range(2)]
        block = s.block()
        U = 2 * K
        view = lambda ap: ap.rearrange("(k p) n -> p k n", p=128)
        part_of = lambda i: slice(K * (1 + i), K * (2 + i))
        own = slice(0, K)

        @block.sync
        def _(sp):
            def load(l):
                b = l % 2
                w_self = view(w_self_t[l])
                for i, w in enumerate((w_fwd, w_bwd)):
                    sp.dma_start(wx_raw[:, b, i], view(w[l])).then_inc(raw_in[b][i], 16)
                    sp.dma_start(ws_raw[:, b, part_of(i)], w_self[:, part_of(i)]).then_inc(raw_in[b][i], 16)
                sp.dma_start(ws_raw[:, b, own], w_self[:, own]).then_inc(raw_in[b][2], 16)

            load(0)
            load(1)
            for l in range(LAYERS):
                sp.wait_ge(lo, 3 * (l + 1))
                if l + 2 < LAYERS:
                    load(l + 2)
                for part in range(2):
                    sp.dma_start(view(wc_dram[l, part, 0:D, :]), ws[:, part, own].bitcast(F32)).then_inc(self_out, 16)
                for u in range(U):
                    sp.wait_ge(lo_o, l * U + u + 1)
                    sp.dma_start(wc_dram[l, :, D + u * 128:D + (u + 1) * 128, :].rearrange("a p n -> p a n"),
                                 wo[:, u % 2].bitcast(F32)).then_inc(out[u % 2], 16)
            sp.wait_ge(self_out, 32 * LAYERS)
            for b in range(2):
                sp.wait_ge(out[b], 16 * LAYERS * U // 2)

        def all_steps():
            for l in range(LAYERS + 1):
                if l < LAYERS:
                    yield "direction", l, 0
                if l >= 1:
                    yield "outputs", l - 1, 1
                if l < LAYERS:
                    yield "direction", l, 1
                    yield "own", l, 2
                    yield "outputs", l, 0

        def free(eng, l, i):
            if l:
                eng.wait_ge(done, (l - 1) * U + (i + 1) * K)

        @block.scalar
        def _(act):
            for what, l, i in all_steps():
                b = l % 2
                if what == "direction":
                    act.wait_ge(raw_in[b][i], 32 * (l // 2 + 1))
                    free(act, l, i)
                    act.activation(wx[:, 0, i], wx_raw[:, b, i], ACT.Copy).then_inc(hi_x, 1)
                elif what == "own":
                    act.wait_ge(raw_in[b][2], 16 * (l // 2 + 1))
                    if l:
                        act.wait_ge(self_out, 32 * l)
                    act.activation(ws[:, 0, own], ws_raw[:, b, own], ACT.Copy).then_inc(hi_self, 1)
                else:
                    for u in range(i * K, (i + 1) * K):
                        n = l * U + u
                        act.wait_ge(done, n + 1)
                        if n >= 2:
                            act.wait_ge(out[u % 2], 16 * (n // 2))
                        act.activation(wo[:, u % 2, 0, :], acc[:, u % 4, :], ACT.Copy).then_inc(hi_o, 1)

        @block.gpsimd
        def _(pool):
            for l in range(LAYERS):
                for i in range(2):
                    pool.wait_ge(raw_in[l % 2][i], 32 * (l // 2 + 1))
                    free(pool, l, i)
                    pool.tensor_copy(ws[:, 0, part_of(i)], ws_raw[:, l % 2, part_of(i)]).then_inc(hi_s, 1)

        @block.vector
        def _(dve):
            for what, l, i in all_steps():
                b = l % 2
                if what == "direction":
                    dve.wait_ge(hi_x, 2 * l + i + 1)
                    dve.tensor_tensor(wx[:, 1, i], wx_raw[:, b, i], wx[:, 0, i].bitcast(F32), ALU.subtract)
                    dve.wait_ge(hi_s, 2 * l + i + 1)
                    dve.tensor_tensor(ws[:, 1, part_of(i)], ws_raw[:, b, part_of(i)], ws[:, 0, part_of(i)].bitcast(F32),
                                      ALU.subtract).then_inc(lo, 1)
                elif what == "own":
                    dve.wait_ge(hi_self, l + 1)
                    dve.tensor_tensor(ws[:, 1, own], ws_raw[:, b, own], ws[:, 0, own].bitcast(F32),
                                      ALU.subtract).then_inc(lo, 1)
                else:
                    for u in range(i * K, (i + 1) * K):
                        dve.wait_ge(hi_o, l * U + u + 1)
                        dve.tensor_tensor(wo[:, u % 2, 1, :], acc[:, u % 4, :], wo[:, u % 2, 0, :].bitcast(F32),
                                          ALU.subtract).then_inc(lo_o, 1)

        @block.tensor
        def _(pe):
            for l in range(LAYERS):
                for u in range(U):
                    n = l * U + u
                    i, m = u // K, u % K
                    if m == 0:
                        pe.wait_ge(lo, 3 * l + i + 1)
                    if n >= 4:
                        pe.wait_ge(lo_o, n - 3)
                    for k in range(K):
                        p = products3(pe, acc[:, u % 4, :],
                                      (wx[:, 0, i, k, rows(m, 128)], wx[:, 1, i, k, rows(m, 128)]),
                                      (ws[:, 0, K * (1 + i) + k, :], ws[:, 1, K * (1 + i) + k, :]),
                                      k == 0, k == K - 1)
                    p.then_inc(done, 1)


def stage_gnn(nc, c, A, AT, at_dram, wc_dram, h_dram):
    CT = 2
    CN = CT * R
    C = T // CT
    UC = 3 * K // 2
    U = C * UC
    RING = 5
    with Stage(nc, "gnn") as s:
        h3 = s.sb("h3", [R, 3, T, D], BF16)
        wc = s.sb("wc", [128, 2, KC, D], F32R)
        rdeg = s.sb("rdeg", [128, 2, N])
        cat = s.sb("cat", [128, 2, 2, KC, CN], F32R)
        mean = s.sb("mean", [128, 2, 2, CN])
        h = s.sb("h", [R, 2, D])
        rest = s.sb("rest", [R, D])
        h3o = s.sb("h3o", [R, 2, 3, D], BF16)
        agg = s.ps("agg", [128, RING, 2, 256])
        hp = s.ps("hp", [R, 2, D])
        first_in = s.sem("first_in")
        last_in = s.sem("last_in")
        wc_in = s.sem("wc_in")
        at_out = s.sem("at_out")
        deg_done = s.sem("deg_done")
        deg_up = s.sem("deg_up")
        chain = s.sem("chain")
        unit_done = s.sem("unit_done")
        mean_ready = s.sem("mean_ready")
        cat_hi = s.sem("cat_hi")
        cat_ready = s.sem("cat_ready")
        rows_done = s.sem("rows_done")
        h_up = s.sem("h_up")
        rest_made = s.sem("rest_made")
        h_split = s.sem("h_split")
        stored = [s.sem(f"stored{b}") for b in range(2)]
        block = s.block()
        mats = (None, AT, A)

        def order():
            for ch in range(C + 1):
                if ch < C:
                    yield "inputs", ch
                if ch >= 1:
                    yield "rows", ch - 1

        @block.sync
        def _(sp):
            split_at = T - CT

            def load(l, a, b, sem):
                src = h_dram[bass.ds(l, 1), a * R:b * R, :, :].rearrange("l (t p) a d -> p (l a) t d", p=R)
                for part in range(3):
                    sp.dma_start(h3[:, part, a:b, :], src[:, part]).then_inc(sem, 16)

            load(0, 0, split_at, first_in)
            load(0, split_at, T, last_in)
            sp.dma_start(at_dram, AT[:]).then_inc(at_out, 16)
            with sp.Fori(0, LAYERS) as l:
                sp.wait_ge(rows_done, l * T + 1)
                for part in range(2):
                    sp.dma_start(wc[:, part].bitcast(F32), wc_dram[bass.ds(l, 1), part].rearrange("l (k p) n -> p (l k) n", p=128))\
                      .then_inc(wc_in, 16)
                for t in range(T):
                    if t == split_at:
                        sp.wait_ge(unit_done, (l + 1) * U)
                        for b in range(2):
                            sp.wait_ge(stored[b], l * (16 * T // 2) + 16 * split_at // 2 + 1)
                        load(l + 1, 0, split_at, first_in)
                    sp.wait_ge(h_split, (l * T + t + 3) * 3)
                    sp.dma_start(h_dram[bass.ds(l + 1, 1), rows(t), :, :].rearrange("l p a d -> p (l a) d"),
                                 h3o[:, t % 2]).then_inc(stored[t % 2], 16)
                for b in range(2):
                    sp.wait_ge(stored[b], (l + 1) * (16 * T // 2) + 1)
                load(l + 1, split_at, T, last_in)
            sp.wait_ge(first_in, 48 * (LAYERS + 1))
            sp.wait_ge(last_in, 48 * (LAYERS + 1))
            sp.wait_ge(at_out, 16)

        @block.tensor
        def _(pe):
            for u in range(6):
                i, (c0, cn) = u // 3, CH[u % 3]
                if u >= 4:
                    pe.wait_ge(deg_up, u - 3)
                for t in range(T):
                    p = pe.matmul(agg[:, u % 4].rearrange("p a n -> p (a n)")[:, 0:cn], c["ones16"][0:R, :],
                                  mats[1 + i][:, t, c0:c0 + cn], start=(t == 0), stop=(t == T - 1))
                p.then_inc(deg_done, 1)
            pe.wait_ge(deg_up, 6)

            def inputs(l, ch):
                for v in range(UC):
                    u = ch * UC + v
                    kind, m2 = v // 2, v % 2
                    pe.wait_ge(cat_ready, l * U + u + 1)
                    for j in range(2):
                        cols = rows(2 * m2 + j, 128)
                        if kind == 0:
                            for i in range(CT):
                                for part in range(3):
                                    p = pe.matmul(agg[:, u % RING, j, i * R:(i + 1) * R],
                                                  h3[:, part, CT * ch + i, cols], c["ident16"][0:R, 0:R],
                                                  start=(j == 0 and i == 0 and part == 0),
                                                  stop=(j == 1 and i == CT - 1 and part == 2),
                                                  skip_group_check=True)
                        else:
                            for t in range(T):
                                for part in range(3):
                                    p = pe.matmul(agg[:, u % RING, j, 0:CN], h3[:, part, t, cols],
                                                  mats[kind][:, t, ch * CN:(ch + 1) * CN],
                                                  start=(j == 0 and t == 0 and part == 0),
                                                  stop=(j == 1 and t == T - 1 and part == 2),
                                                  skip_group_check=True)
                    p.then_inc(unit_done, 1)

            def new_rows(l, ch):
                pe.wait_ge(cat_ready, l * U + (ch + 1) * UC + RING)
                if ch == 0:
                    pe.wait_ge(wc_in, (l + 1) * 32)
                for i in range(CT):
                    t = CT * ch + i
                    pe.wait_ge(h_up, l * T + t + 1)
                    for k in range(KC):
                        p = products3(pe, hp[:, t % 2, :],
                                      (cat[:, ch % 2, 0, k, i * R:(i + 1) * R], cat[:, ch % 2, 1, k, i * R:(i + 1) * R]),
                                      (wc[:, 0, k, :], wc[:, 1, k, :]), k == 0, k == KC - 1)
                    p.then_inc(rows_done, 1)

            with pe.Fori(0, LAYERS) as l:
                pe.wait_ge(first_in, (l + 1) * 48)
                pe.wait_ge(last_in, (l + 1) * 48)
                for what, ch in order():
                    inputs(l, ch) if what == "inputs" else new_rows(l, ch)

        @block.scalar
        def _(act):
            def high_parts(l, ch):
                act.wait_ge(rows_done, l * T + max(0, (ch - 1) * CT) + 1)
                for v in range(UC):
                    u = ch * UC + v
                    kind, m2 = v // 2, v % 2
                    dst = cat[:, ch % 2, 0, kind * K + 2 * m2:kind * K + 2 * m2 + 2, :]
                    if kind == 0:
                        act.wait_ge(unit_done, l * U + u + 1)
                        act.activation(dst, agg[:, u % RING, :, 0:CN], ACT.Copy).then_inc(cat_hi, 1)
                    else:
                        act.wait_ge(mean_ready, l * (U - 2 * C) + ch * (UC - 2) + v - 1)
                        act.activation(dst, mean[:, v % 2], ACT.Copy).then_inc(cat_hi, 1)

            def up(l, ch):
                for i in range(CT):
                    t = CT * ch + i
                    act.wait_ge(rows_done, l * T + t + 1 + 1)
                    act.wait_ge(h_split, (l * T + t + 1) * 3)
                    act.activation(h[:, t % 2, :], hp[:, t % 2, :], ACT.Relu).then_inc(h_up, 1)

            with act.Fori(0, LAYERS) as l:
                for what, ch in order():
                    high_parts(l, ch) if what == "inputs" else up(l, ch)

        @block.vector
        def _(dve):
            link = Chain(dve, chain)
            for u in range(6):
                i, (c0, cn) = u // 3, CH[u % 3]
                dve.wait_ge(deg_done, u + 1)
                dve.tensor_scalar(rdeg[:, i, c0:c0 + cn], agg[:, u % 4].rearrange("p a n -> p (a n)")[:, 0:cn],
                                  1.0, None, ALU.max).then_inc(deg_up, 1)
            dve.wait_ge(deg_up, 6)
            link(dve.reciprocal(rdeg[:], rdeg[:]))
            dve.sem_inc(cat_ready, RING)
            for sem in (rows_done, *stored):
                dve.sem_inc(sem, 1)
            dve.sem_inc(h_up, 2)

            def low_parts(l, ch):
                cols = slice(ch * CN, (ch + 1) * CN)
                dve.wait_ge(rows_done, l * T + max(0, (ch - 1) * CT) + 1)
                for v in range(UC):
                    u = ch * UC + v
                    kind, m2 = v // 2, v % 2
                    lo, hi = (cat[:, ch % 2, part, kind * K + 2 * m2:kind * K + 2 * m2 + 2, :] for part in (1, 0))
                    if kind == 0:
                        dve.wait_ge(cat_hi, l * U + u + 1)
                        dve.tensor_tensor(lo, agg[:, u % RING, :, 0:CN], hi.bitcast(F32), ALU.subtract)\
                           .then_inc(cat_ready, 1)
                        continue
                    dve.wait_ge(unit_done, l * U + u + 1)
                    dve.tensor_tensor(mean[:, v % 2], agg[:, u % RING, :, 0:CN],
                                      rdeg[:, kind - 1, cols].unsqueeze(1).to_broadcast([128, 2, CN]), ALU.mult)\
                       .then_inc(mean_ready, 1)
                    dve.wait_ge(mean_ready, l * (U - 2 * C) + ch * (UC - 2) + v - 1)
                    dve.wait_ge(cat_hi, l * U + u + 1)
                    dve.tensor_tensor(lo, mean[:, v % 2], hi.bitcast(F32), ALU.subtract).then_inc(cat_ready, 1)

            def split_rows(l, ch):
                for i in range(CT):
                    t = CT * ch + i
                    b = t % 2
                    dve.wait_ge(h_up, l * T + t + 1 + 2)
                    dve.wait_ge(stored[b], l * (16 * T // 2) + 16 * (t // 2) + 1)
                    dve.tensor_copy(h3o[:, b, 0, :], h[:, b, :]).then_inc(h_split, 1)
                    dve.wait_ge(h_split, (l * T + t) * 3 + 1 + 6)
                    dve.tensor_tensor(rest[:], h[:, b, :], h3o[:, b, 0, :], ALU.subtract).then_inc(rest_made, 1)
                    dve.wait_ge(rest_made, l * T + t + 1)
                    dve.tensor_copy(h3o[:, b, 1, :], rest[:]).then_inc(h_split, 1)
                    dve.wait_ge(h_split, (l * T + t) * 3 + 2 + 6)
                    dve.tensor_tensor(h3o[:, b, 2, :], rest[:], h3o[:, b, 1, :], ALU.subtract).then_inc(h_split, 1)

            dve.sem_inc(h_split, 6)
            with dve.Fori(0, LAYERS) as l:
                for what, ch in order():
                    low_parts(l, ch) if what == "inputs" else split_rows(l, ch)


E = 8
SLOT_ROWS = 105
SLOT_TILES = 4
CHUNK = SLOT_ROWS * SLOT_TILES
CHUNKS = -(-N // CHUNK)


def max_passes(top):
    return E + top * N // CHUNK


NEAR = math.log1p(-0.02)


def stage_route(nc, c, name, terms, gate_t, gate_b, top, x_out, xn_out, fm, slot_i, weight, table, token_dram):
    NP = max_passes(top)
    NT = len(terms)
    DEEP = 5
    with Stage(nc, name) as s:
        xin = [s.sb(f"xin{i}", [R, DEEP, D], ap.dtype) for i, ap in enumerate(terms)]
        xs = s.sb("x", [R, T, D])
        xn = s.sb("xn", [R, T, D])
        g_raw = s.sb("g_raw", [128, K, E])
        g2 = s.sb("g2", [128, 2, K, E], F32R)
        gb = s.sb("gb", [R, E])
        stats = s.sb("stats", [R, T, 6])
        mv = s.sb("mv", [R, T, 2])
        rstd, var, root = (s.sb(n, [R, T]) for n in ("rstd", "var", "root"))
        iota_i = s.sb("iota_i", [R, T, E], I32)
        iota = s.sb("iota", [R, T, E])
        tok = s.sb("tok", [R, T], I32)
        tri = s.sb("tri", [R, R])
        zero = s.sb("zero", [SLOT_ROWS, (NP + 1) * SLOT_TILES], I32)
        sc = s.sb("sc", [R, T, E])
        ex = s.sb("ex", [R, T, E])
        masked = s.sb("masked", [R, T, E])
        lgs = s.sb("lgs", [R, T, E])
        lmx = s.sb("lmx", [R, T])
        t1 = s.sb("t1", [R, T, E])
        oh = s.sb("oh", [R, top, T, E])
        sel = s.sb("sel", [R, T, E])
        slots = s.sb("slots", [R, T, E])
        carry = s.sb("carry", [R, T + 1, E])
        mx, sm, id1 = (s.sb(n, [R, T]) for n in ("mx", "sm", "id1"))
        slot_f = s.sb("slot_f", [R, top, T])
        npass = s.sb("npass", [R, E])
        ends = s.sb("ends", [R, E])
        start = s.sb("start", [R, E])
        cmp_ = s.sb("cmp", [1, NP, E])
        num_i = s.sb("num_i", [1, NP], I32)
        num = s.sb("num", [1, NP])
        row_e, row_b, left = (s.sb(n, [1, NP]) for n in ("row_e", "row_b", "left"))
        tp = s.ps("tp", [128, 2, K, 128])
        lg = s.ps("lg", [R, T, E])
        pre = s.ps("pre", [R, 2, T * E])
        in_ = [s.sem(f"in{b}") for b in range(DEEP)]
        w_in = s.sem("w_in")
        chain = s.sem("chain")
        summed = s.sem("summed")
        moments = s.sem("moments")
        rooted = s.sem("rooted")
        xn_ready = s.sem("xn_ready")
        turned = s.sem("turned")
        fm_hi = s.sem("fm_hi")
        fm_ready = s.sem("fm_ready")
        gate_ready = s.sem("gate_ready")
        logits = s.sem("logits")
        less = s.sem("less")
        exped = s.sem("exped")
        iotas = s.sem("iotas")
        sel_ready = s.sem("sel_ready")
        ranked = s.sem("ranked")
        x_stored = s.sem("x_stored")
        zeroed = s.kept_sem("zeroed")
        slots_ready = s.sem("slots_ready")
        scattered = s.kept_sem("scattered")
        block = s.block()
        bc = lambda ap: ap.unsqueeze(2).to_broadcast([R, T, E])

        @block.sync
        def _(sp):
            sp.dma_start(g_raw[:], gate_t.rearrange("(k p) n -> p k n", p=128)).then_inc(w_in, 16)
            if gate_b is not None:
                sp.dma_start(gb[:], gate_b.partition_broadcast(R)).then_inc(w_in, 16)
            for t in range(T):
                if t >= DEEP:
                    sp.wait_ge(summed, t - DEEP + 1)
                for i, ap in enumerate(terms):
                    sp.dma_start(xin[i][:, t % DEEP, :], ap[rows(t), :]).then_inc(in_[t % DEEP], 16)
            sp.wait_ge(summed, T)
            sp.dma_start(x_out.rearrange("(t p) d -> p t d", p=R), xs[:]).then_inc(x_stored, 16)
            sp.wait_ge(xn_ready, T)
            sp.dma_start(xn_out.rearrange("(t p) d -> p t d", p=R), xn[:]).then_inc(x_stored, 16)
            sp.wait_ge(x_stored, 32)

        @block.gpsimd
        def _(pool):
            pool.iota(iota_i[:], pattern=[[0, T], [1, E]], base=0, channel_multiplier=0).then_inc(iotas, 1)
            pool.iota(tok[:], pattern=[[R, T]], base=0, channel_multiplier=1).then_inc(iotas, 1)
            pool.iota(num_i[:], pattern=[[1, NP]], base=0, channel_multiplier=0).then_inc(iotas, 1)
            pool.memset(zero[:], 0).then_inc(iotas, 1)
            pool.memset(tri[:], 1.0).then_inc(iotas, 1)
            pool.wait_ge(iotas, 5)
            pool.affine_select(out=tri[:], in_=tri[:], compare_op=ALU.is_gt, fill=0.0, base=0,
                               pattern=[[1, R]], channel_multiplier=-1).then_inc(iotas, 1)
            pool.dma_start(token_dram.rearrange("(p n) a -> p (n a)", p=SLOT_ROWS), zero[:]).then_inc(zeroed, 16)
            pool.wait_ge(zeroed, 16)
            pool.wait_ge(slots_ready, 1)
            for i in range(top):
                for t in range(T):
                    pool.indirect_dma_start(out=token_dram, out_offset=bass.IndirectOffsetOnAxis(
                        ap=slot_i[:, i, t:t + 1], axis=0), in_=tok[:, t:t + 1], in_offset=None).then_inc(scattered, 16)
            pool.wait_ge(scattered, 16 * top * T)

        @block.tensor
        def _(pe):
            for t in range(T):
                pe.wait_ge(xn_ready, t + 1)
                if t >= 2:
                    pe.wait_ge(fm_ready, t - 1)
                for k in range(K):
                    p = pe.transpose(tp[:, t % 2, k, 0:R], xn[:, t, rows(k, 128)], c["ident"][0:R, 0:R])
                p.then_inc(turned, 1)
            pe.wait_ge(gate_ready, 1)
            pe.wait_ge(fm_ready, T)
            for t in range(T):
                for k in range(K):
                    p = products3(pe, lg[:, t, :], (fm[:, 0, k, rows(t)], fm[:, 1, k, rows(t)]),
                                  (g2[:, 0, k, :], g2[:, 1, k, :]), k == 0, k == K - 1)
            p.then_inc(logits, 1)
            pe.wait_ge(sel_ready, 1)
            pe.wait_ge(iotas, 6)
            flat = sel[:].rearrange("p t e -> p (t e)")
            pe.matmul(pre[:, 0, :], tri[:], flat, start=True, stop=True)
            pe.matmul(pre[:, 1, :], c["ones"][0:R, 0:R], flat, start=True, stop=True).then_inc(ranked, 1)

        @block.scalar
        def _(act):
            act.wait_ge(moments, 1)
            act.activation(root[:], var[:], ACT.Sqrt).then_inc(rooted, 1)
            for t in range(T):
                act.wait_ge(turned, t + 1)
                act.activation(fm[:, 0, :, rows(t)], tp[:, t % 2, :, 0:R], ACT.Copy).then_inc(fm_hi, 1)
            for n in range(3 if top == 2 else 0):
                act.wait_ge(less, n + 1)
                act.activation(ex[:], t1[:], ACT.Exp).then_inc(exped, 1)

        @block.vector
        def _(dve):
            link = Chain(dve, chain)
            for t in range(T):
                dve.wait_ge(in_[t % DEEP], 16 * NT * (t // DEEP + 1))
                for i in range(1, NT):
                    d = dve.tensor_tensor(xs[:, t, :], xin[0][:, t % DEEP, :] if i == 1 else xs[:, t, :],
                                          xin[i][:, t % DEEP, :], ALU.add)
                    if i < NT - 1:
                        link(d)
                d.then_inc(summed, 1)
            row_moments(dve, link, xs, stats, mv, lambda t: dve.wait_ge(summed, t + 1))
            link(dve.tensor_scalar(var[:], mv[:, :, 1], 1e-5, None, ALU.add))
            dve.sem_inc(moments, 1)
            dve.wait_ge(rooted, 1)
            inverse_root(dve, link, rstd[:], var[:], root[:])
            for t in range(T):
                dve.tensor_scalar(xn[:, t, :], xs[:, t, :], mv[:, t, 0:1], rstd[:, t:t + 1],
                                  ALU.subtract, ALU.mult).then_inc(xn_ready, 1)
            dve.wait_ge(w_in, 16 if gate_b is None else 32)
            link(dve.tensor_copy(g2[:, 0], g_raw[:]))
            dve.tensor_tensor(g2[:, 1], g_raw[:], g2[:, 0].bitcast(F32), ALU.subtract).then_inc(gate_ready, 1)
            dve.wait_ge(iotas, 6)
            dve.tensor_copy(iota[:], iota_i[:])
            link(dve.tensor_copy(num[:], num_i[:]))
            for t in range(T):
                dve.wait_ge(fm_hi, t + 1)
                dve.tensor_tensor(fm[:, 1, :, rows(t)], tp[:, t % 2, :, 0:R],
                                  fm[:, 0, :, rows(t)].bitcast(F32), ALU.subtract).then_inc(fm_ready, 1)
            dve.wait_ge(logits, 1)

            def first_of_max(i):
                link(dve.tensor_reduce(lmx[:], masked[:], AX, ALU.max))
                link(dve.tensor_tensor(t1[:], masked[:], bc(lmx[:]), ALU.is_lt))
                link(dve.scalar_tensor_tensor(out=t1[:], in0=t1[:], scalar=float(E), in1=iota[:],
                                              op0=ALU.mult, op1=ALU.add))
                link(dve.tensor_reduce(id1[:], t1[:], AX, ALU.min))
                link(dve.tensor_tensor(oh[:, i], iota[:], bc(id1[:]), ALU.is_equal))
                if top == 2:
                    link(dve.tensor_tensor(t1[:], oh[:, i], sc[:], ALU.mult))
                    link(dve.tensor_reduce(mx[:], t1[:], AX, ALU.add))

            def weigh(i, kept=None):
                link(dve.tensor_tensor(t1[:], sc[:], bc(mx[:]), ALU.subtract))
                dve.sem_inc(less, 1)
                dve.wait_ge(exped, i + 2)
                link(dve.tensor_tensor(t1[:], lgs[:], bc(lmx[:]), ALU.subtract))
                link(dve.tensor_scalar(t1[:], t1[:], NEAR, None, ALU.is_ge))
                if kept is not None:
                    link(dve.tensor_tensor(t1[:], t1[:], kept, ALU.mult))
                link(dve.tensor_tensor(t1[:], t1[:], ex[:], ALU.mult))
                link(dve.tensor_reduce(sm[:], t1[:], AX, ALU.add))
                link(dve.reciprocal(weight[:, i, :], sm[:]))

            if gate_b is not None:
                link(dve.tensor_tensor(lgs[:], lg[:], gb[:].unsqueeze(1).to_broadcast([R, T, E]), ALU.add))
            else:
                link(dve.tensor_copy(lgs[:], lg[:]))
            link(dve.tensor_copy(masked[:], lgs[:]))
            if top == 2:
                link(dve.tensor_reduce(mx[:], lgs[:], AX, ALU.max))
                link(dve.tensor_tensor(t1[:], lgs[:], bc(mx[:]), ALU.subtract))
                dve.sem_inc(less, 1)
                dve.wait_ge(exped, 1)
                link(dve.tensor_reduce(sm[:], ex[:], AX, ALU.add))
                link(dve.reciprocal(sm[:], sm[:]))
                link(dve.tensor_tensor(sc[:], ex[:], bc(sm[:]), ALU.mult))
                first_of_max(0)
                weigh(0)
                link(dve.scalar_tensor_tensor(out=masked[:], in0=oh[:, 0], scalar=-1e30, in1=lgs[:],
                                              op0=ALU.mult, op1=ALU.add))
                first_of_max(1)
                link(dve.tensor_scalar(slots[:], oh[:, 0], -1.0, 1.0, ALU.mult, ALU.add))
                weigh(1, kept=slots[:])
                link(dve.tensor_tensor(sel[:], oh[:, 0], oh[:, 1], ALU.add))
            else:
                first_of_max(0)
                dve.memset(weight[:, 0, :], 1.0)
                link(dve.tensor_copy(sel[:], oh[:, 0]))
            dve.sem_inc(sel_ready, 1)
            link(dve.memset(carry[:, 0, :], 0.0))
            dve.wait_ge(ranked, 1)
            totals = pre[:, 1, :].rearrange("p (t e) -> p t e", e=E)
            for t in range(T):
                link(dve.tensor_tensor(carry[:, t + 1, :], carry[:, t, :], totals[:, t, :], ALU.add))
            link(dve.tensor_tensor(slots[:], pre[:, 0, :].rearrange("p (t e) -> p t e", e=E), carry[:, 0:T, :], ALU.add))
            count = carry[:, T, :]
            link(dve.tensor_scalar(npass[:], count, 0.0, None, ALU.is_gt))
            for q in range(1, CHUNKS):
                link(dve.tensor_scalar(ends[:], count, float(q * CHUNK), None, ALU.is_gt))
                link(dve.tensor_tensor(npass[:], npass[:], ends[:], ALU.add))
            link(dve.tensor_copy(ends[:], npass[:]))
            for e in range(1, E):
                link(dve.tensor_tensor(ends[:, e:e + 1], ends[:, e - 1:e], npass[:, e:e + 1], ALU.add))
            link(dve.tensor_tensor(start[:], ends[:], npass[:], ALU.subtract))
            link(dve.tensor_scalar(start[:], start[:], float(CHUNK), None, ALU.mult))
            link(dve.tensor_tensor(slots[:], slots[:], start[:].unsqueeze(1).to_broadcast([R, T, E]), ALU.add))
            for i in range(top):
                link(dve.tensor_tensor(t1[:], slots[:], oh[:, i], ALU.mult))
                link(dve.tensor_reduce(slot_f[:, i, :], t1[:], AX, ALU.add))
            link(dve.tensor_copy(slot_i[:], slot_f[:]))
            dve.sem_inc(slots_ready, 1)
            link(dve.tensor_tensor(cmp_[:], ends[0:1, :].unsqueeze(1).to_broadcast([1, NP, E]),
                                   num[:].unsqueeze(2).to_broadcast([1, NP, E]), ALU.is_le))
            link(dve.tensor_reduce(row_e[:], cmp_[:], AX, ALU.add))
            link(dve.tensor_scalar(row_b[:], row_e[:], float(E), None, ALU.is_lt))
            link(dve.tensor_tensor(ends[:], count, start[:], ALU.add))
            link(dve.tensor_tensor(cmp_[:], iota[0:1, 0:1, :].to_broadcast([1, NP, E]),
                                   row_e[:].unsqueeze(2).to_broadcast([1, NP, E]), ALU.is_equal))
            link(dve.tensor_tensor(cmp_[:], cmp_[:], ends[0:1, :].unsqueeze(1).to_broadcast([1, NP, E]), ALU.mult))
            link(dve.tensor_reduce(left[:], cmp_[:], AX, ALU.add))
            link(dve.scalar_tensor_tensor(out=left[:], in0=num[:], scalar=-float(CHUNK), in1=left[:],
                                          op0=ALU.mult, op1=ALU.add))
            link(dve.tensor_scalar(left[:], left[:], CHUNK / 2, 1.0, ALU.is_gt, ALU.add))
            link(dve.tensor_tensor(row_b[:], row_b[:], left[:], ALU.mult))
            link(dve.tensor_scalar(row_e[:], row_e[:], float(E - 1), None, ALU.min))
            link(dve.memset(table[:], 0))
            link(dve.tensor_copy(table[0:1, 0, 0:NP], row_e[:]))
            link(dve.tensor_copy(table[0:1, 1, 0:NP], row_b[:]))


def stage_experts(nc, c, name, top, F, func, w1, w3, w2, xn_dram, token_dram, table, y_dram):
    NP = max_passes(top)
    FQ = 2
    NQ = F // (128 * FQ)
    UNROLL = 1 if NQ % 2 == 0 else 2
    NF = FQ * NQ
    U = SLOT_TILES + 2 * NF
    RING = 4
    assert U % RING == 0 and NP % UNROLL == 0
    with Stage(nc, name) as s:
        tok = s.sb("tok", [SLOT_ROWS, SLOT_TILES], I32)
        xg = s.sb("xg", [SLOT_ROWS, SLOT_TILES, D])
        fm = s.sb("fm", [128, 2, K, CHUNK], F32R)
        wa_raw = s.sb("wa_raw", [128, 2, 2, K, FQ * 128])
        wa = s.sb("wa", [128, 2, 2, 2, K, FQ * 128], F32R)
        wb_raw = s.sb("wb_raw", [128, 2, FQ, D])
        wb = s.sb("wb", [128, 2, 2, FQ, D], F32R)
        g = s.sb("g", [128, 2, CHUNK])
        hv = s.sb("hv", [128, 2, CHUNK])
        hT = s.sb("hT", [128, 2, 2, CHUNK], F32R)
        y = s.sb("y", [SLOT_ROWS, SLOT_TILES, D])
        zero = s.sb("zero", [SLOT_ROWS, SLOT_TILES, D])
        zeroed = s.sem("zeroed")
        ring = s.ps("ring", [128, RING, 512])
        yp = s.ps("yp", [SLOT_ROWS, SLOT_TILES, D])
        tok_in = s.kept_sem("tok_in")
        gathered = s.kept_sem("gathered")
        carried = s.sem("carried")
        turned = s.sem("turned")
        fm_hi = s.sem("fm_hi")
        fm_ready = s.sem("fm_ready")
        raw_in = [s.sem(f"raw_in{b}") for b in range(2)]
        w_hi = s.sem("w_hi")
        w_ready = s.sem("w_ready")
        unit_done = s.sem("unit_done")
        g_ready = s.sem("g_ready")
        hv_ready = s.sem("hv_ready")
        h_hi = s.sem("h_hi")
        h_ready = s.sem("h_ready")
        part_used = s.sem("part_used")
        y_ready = s.sem("y_ready")
        y_out = s.kept_sem("y_out")
        block = s.block()

        def passes(eng, body):
            with eng.Fori(0, NP // UNROLL) as j:
                for o in range(UNROLL):
                    i = j * UNROLL + o
                    used = eng.value_load(table[0:1, 1, bass.ds(i, 1)], min_val=0, max_val=2)
                    with eng.If(used > 1):
                        body(i, o, j, SLOT_TILES)
                    with eng.Else():
                        with eng.If(used > 0):
                            body(i, o, j, SLOT_TILES // 2)
                    eng.nop()

        def loads(eng, body, otherwise=None):
            with eng.Fori(0, NP // UNROLL) as j:
                for o in range(UNROLL):
                    i = j * UNROLL + o
                    used = eng.value_load(table[0:1, 1, bass.ds(i, 1)], min_val=0, max_val=2)
                    with eng.If(used > 0):
                        body(i, o)
                    if otherwise is not None:
                        with eng.Else():
                            otherwise(i)
                    eng.nop()

        def rows_leave(eng, copy, i, part):
            eng.wait_ge(part_used, (i + 1) * NF + 2 * FQ)
            eng.wait_ge(tok_in, i * 16 + 32)
            copy(y[:, part, :], yp[:, part, :]).then_inc(y_ready, 1)

        def raw_total(i, o, j, q):
            return ((j + (o * NQ + q) // 2 if UNROLL == 2 else i * (NQ // 2) + q // 2) + 1) * 48

        def use_before(n):
            return n * FQ + FQ

        def parity(q, o):
            return (o * NQ + q) % 2


        @block.sync
        def _(sp):
            def load(e, q, b):
                for j, w in enumerate((w1, w3)):
                    src = w[bass.ds(e, 1), :, q * FQ * 128:(q + 1) * FQ * 128]
                    sp.dma_start(wa_raw[:, b, j], src.rearrange("e (k p) f -> p (e k) f", p=128)).then_inc(raw_in[b], 16)
                src = w2[bass.ds(e, 1), q * FQ * 128:(q + 1) * FQ * 128, :]
                sp.dma_start(wb_raw[:, b], src.rearrange("e (k p) f -> p (e k) f", p=128)).then_inc(raw_in[b], 16)

            def body(i, o):
                e = sp.value_load(table[0:1, 0, bass.ds(i, 1)], min_val=0, max_val=E - 1)
                after = sp.value_load(table[0:1, 0, bass.ds(i + 1, 1)], min_val=0, max_val=E - 1)
                for q in range(1, NQ + 1):
                    sp.wait_ge(w_ready, i * NQ + q + 1)
                    load(e if q < NQ else after, q % NQ, parity(q, o))

            load(sp.value_load(table[0:1, 0, 0:1], min_val=0, max_val=E - 1), 0, 0)
            loads(sp, body)

        @block.gpsimd
        def _(pool):
            def gather(i):
                for k in range(SLOT_TILES):
                    pool.indirect_dma_start(out=xg[:, k, :], out_offset=None, in_=xn_dram,
                                            in_offset=bass.IndirectOffsetOnAxis(ap=tok[:, k:k + 1], axis=0))\
                        .then_inc(gathered, 16)

            def tokens(i):
                return token_dram[bass.ds(i * CHUNK, CHUNK), :].rearrange("(s p) a -> p (s a)", p=SLOT_ROWS)

            def rows_of(i):
                return y_dram[bass.ds(i * CHUNK, CHUNK), :].rearrange("(s p) d -> p s d", p=SLOT_ROWS)

            def body(i, o):
                pool.wait_ge(turned, (i + 1) * SLOT_TILES + 1)
                pool.dma_start(tok[:], tokens(i + 1), allow_slow_non_contiguous=True).then_inc(tok_in, 16)
                pool.wait_ge(tok_in, i * 16 + 32)
                carry_wait(pool, c, carried, i + 1)
                gather(i + 1)
                pool.wait_ge(gathered, (i + 2) * (16 * SLOT_TILES))
                pool.wait_ge(y_ready, (i + 1) * 2 + 1)
                pool.dma_start(rows_of(i), y[:]).then_inc(y_out, 16)
                pool.wait_ge(y_out, i * 16 + 16)

            def none(i):
                pool.dma_start(rows_of(i), zero[:]).then_inc(y_out, 16)
                pool.wait_ge(y_out, i * 16 + 16)

            pool.dma_start(tok[:], tokens(0), allow_slow_non_contiguous=True).then_inc(tok_in, 16)
            pool.wait_ge(tok_in, 16)
            gather(0)
            pool.wait_ge(zeroed, 2)
            loads(pool, body, none)

        @block.tensor
        def _(pe):
            def body(i, o, j_, tiles):
                W, per = tiles * SLOT_ROWS, SLOT_TILES // tiles
                pe.wait_ge(gathered, (i + 1) * (16 * SLOT_TILES))
                for u in range(tiles):
                    pe.wait_ge(fm_ready, i * SLOT_TILES + 1)
                    if u == 0:
                        pe.wait_ge(h_ready, i * NF + 1)
                    for k in range(K):
                        p = pe.transpose(ring[:, u, k * 128:k * 128 + SLOT_ROWS], xg[:, u, rows(k, 128)],
                                         c["ident"][0:SLOT_ROWS, 0:SLOT_ROWS])
                    p.then_inc(turned, per)

                def hidden(f):
                    q, b = f // FQ, parity(f // FQ, o)
                    if f % FQ == 0:
                        pe.wait_ge(w_ready, i * NQ + q + 1 + 2)
                    if f == 0:
                        pe.wait_ge(fm_ready, (i + 1) * SLOT_TILES + 1)
                    if f >= 2:
                        pe.wait_ge(hv_ready, i * NF + f - 1 + 1)
                    for j in range(2):
                        for k in range(K):
                            cols = rows(f % FQ, 128)
                            p = products3(pe, ring[:, (2 * f + j) % RING, 0:W],
                                          (wa[:, b, j, 0, k, cols], wa[:, b, j, 1, k, cols]),
                                          (fm[:, 0, k, 0:W], fm[:, 1, k, 0:W]), k == 0, k == K - 1)
                        p.then_inc(unit_done, 1)

                def output(f):
                    b = parity(f // FQ, o)
                    pe.wait_ge(h_ready, i * NF + f + 1 + 1)
                    if f == 0:
                        pe.wait_ge(y_ready, i * 2 + 1)
                    for u in range(tiles):
                        p = products3(pe, yp[:, u, :], (hT[:, f % 2, 0, rows(u, SLOT_ROWS)], hT[:, f % 2, 1, rows(u, SLOT_ROWS)]),
                                      (wb[:, b, 0, f % FQ, :], wb[:, b, 1, f % FQ, :]), f == 0, f == NF - 1)
                    p.then_inc(part_used, 1)

                hidden(0)
                for f in range(NF):
                    if f + 1 < NF:
                        hidden(f + 1)
                    output(f)
            passes(pe, body)

        @block.scalar
        def _(act):
            def split_high(b, total, used):
                act.wait_ge(raw_in[b], total)
                act.wait_ge(part_used, used)
                act.activation(wa[:, b, :, 0], wa_raw[:, b], ACT.Copy).then_inc(w_hi, 1)
                act.activation(wb[:, b, 0], wb_raw[:, b], ACT.Copy).then_inc(w_hi, 1)

            def body(i, o, j_, tiles):
                W, per = tiles * SLOT_ROWS, SLOT_TILES // tiles
                act.wait_ge(unit_done, i * (2 * NF) + 1)
                for u in range(tiles):
                    act.wait_ge(turned, i * SLOT_TILES + (u + 1) * per + 1)
                    act.activation(fm[:, 0, :, rows(u, SLOT_ROWS)],
                                   ring[:, u, :].rearrange("p (k n) -> p k n", k=K)[:, :, 0:SLOT_ROWS], ACT.Copy)\
                       .then_inc(fm_hi, per)
                for f in range(NF):
                    b = f % 2
                    act.wait_ge(unit_done, i * (2 * NF) + 2 * f + 1 + 1)
                    act.wait_ge(hv_ready, i * NF + max(0, f - 1) + 1)
                    act.activation(g[:, b, 0:W], ring[:, (2 * f) % RING, 0:W], func).then_inc(g_ready, 1)
                    act.wait_ge(hv_ready, i * NF + f + 1 + 1)
                    act.wait_ge(part_used, i * NF + max(0, f - 1) + 2 * FQ)
                    act.activation(hT[:, b, 0, 0:W], hv[:, b, 0:W], ACT.Copy).then_inc(h_hi, 1)
                    if f % FQ == 0:
                        q = f // FQ + 1
                        split_high(parity(q, o), raw_total(i, o, j_, q), use_before(i * NQ + q))
                rows_leave(act, lambda to, of: act.activation(to, of, ACT.Copy), i, slice(0, tiles // 2))

            act.wait_ge(zeroed, 2)
            split_high(0, 48, FQ)
            passes(act, body)

        @block.vector
        def _(dve):
            dve.memset(y[:], 0.0).then_inc(zeroed, 1)
            dve.memset(zero[:], 0.0).then_inc(zeroed, 1)
            for sem in (turned, unit_done, hv_ready, h_ready, fm_ready, y_ready, carried):
                dve.sem_inc(sem, 1)
            dve.sem_inc(w_ready, 2)
            dve.sem_inc(part_used, 2 * FQ)

            def split_low(b, made):
                dve.wait_ge(w_hi, made)
                dve.tensor_tensor(wa[:, b, :, 1], wa_raw[:, b], wa[:, b, :, 0].bitcast(F32), ALU.subtract)
                dve.tensor_tensor(wb[:, b, 1], wb_raw[:, b], wb[:, b, 0].bitcast(F32), ALU.subtract).then_inc(w_ready, 1)

            def body(i, o, j_, tiles):
                W, per = tiles * SLOT_ROWS, SLOT_TILES // tiles
                for u in range(tiles):
                    dve.wait_ge(fm_hi, i * SLOT_TILES + (u + 1) * per)
                    dve.tensor_tensor(fm[:, 1, :, rows(u, SLOT_ROWS)],
                                      ring[:, u, :].rearrange("p (k n) -> p k n", k=K)[:, :, 0:SLOT_ROWS],
                                      fm[:, 0, :, rows(u, SLOT_ROWS)].bitcast(F32), ALU.subtract).then_inc(fm_ready, per)
                for f in range(NF):
                    b = f % 2
                    dve.wait_ge(g_ready, i * NF + f + 1)
                    dve.wait_ge(unit_done, i * (2 * NF) + 2 * f + 2 + 1)
                    dve.wait_ge(h_ready, i * NF + max(0, f - 1) + 1)
                    dve.tensor_tensor(hv[:, b, 0:W], g[:, b, 0:W], ring[:, (2 * f + 1) % RING, 0:W], ALU.mult)\
                       .then_inc(hv_ready, 1)
                    dve.wait_ge(h_hi, i * NF + f + 1)
                    dve.tensor_tensor(hT[:, b, 1, 0:W], hv[:, b, 0:W], hT[:, b, 0, 0:W].bitcast(F32), ALU.subtract)\
                       .then_inc(h_ready, 1)
                    if f % FQ == 0:
                        q = f // FQ + 1
                        split_low(parity(q, o), (i * NQ + q + 1) * 2)
                rows_leave(dve, dve.tensor_copy, i, slice(tiles // 2, tiles))

            dve.wait_ge(zeroed, 2)
            split_low(0, 2)
            passes(dve, body)


def stage_combine(nc, c, name, top, x_dram, y_dram, slot_i, weight, extra, out):
    with Stage(nc, name) as s:
        yt = s.sb("yt", [R, top, T, D])
        xs = s.sb("xs", [R, T, D])
        ex = s.sb("ex", [R, T, D]) if extra is not None else None
        x_in = s.sem("x_in")
        y_in = [s.kept_sem(f"y_in{t}") for t in range(T)]
        acc = s.sem("acc")
        stored = s.sem("stored")
        block = s.block()
        view = lambda ap: ap.rearrange("(t p) d -> p t d", p=R)
        steps = top + (extra is not None)

        @block.gpsimd
        def _(pool):
            for t in range(T):
                for i in range(top):
                    pool.indirect_dma_start(out=yt[:, i, t, :], out_offset=None, in_=y_dram,
                                            in_offset=bass.IndirectOffsetOnAxis(ap=slot_i[:, i, t:t + 1], axis=0))\
                        .then_inc(y_in[t], 16)
            for t in range(T):
                pool.wait_ge(y_in[t], 16 * top)

        @block.sync
        def _(sp):
            sp.dma_start(xs[:], view(x_dram)).then_inc(x_in, 16)
            if extra is not None:
                sp.dma_start(ex[:], view(extra)).then_inc(x_in, 16)
            for j in range(T // 2):
                sp.wait_ge(acc, steps * (2 * j + 2))
                sp.dma_start(view(out)[:, 2 * j:2 * j + 2, :], xs[:, 2 * j:2 * j + 2, :]).then_inc(stored, 16)
            sp.wait_ge(stored, 16 * T // 2)

        @block.vector
        def _(dve):
            dve.wait_ge(x_in, 16 * (1 + (extra is not None)))
            for t in range(T):
                dve.wait_ge(y_in[t], 16 * top)
                for i in range(steps):
                    if i:
                        dve.wait_ge(acc, t * steps + i)
                    if i < top:
                        d = dve.scalar_tensor_tensor(out=xs[:, t, :], in0=yt[:, i, t, :], scalar=weight[:, i, t:t + 1],
                                                     in1=xs[:, t, :], op0=ALU.mult, op1=ALU.add)
                    else:
                        d = dve.tensor_tensor(xs[:, t, :], xs[:, t, :], ex[:, t, :], ALU.add)
                    d.then_inc(acc, 1)


def by_part(v):
    return v.rearrange("(k p) -> p k", p=128)


def stage_turn(nc, c, name, x_dram, norms, out_dram, gain, bias, fm):
    with Stage(nc, name) as s:
        xs = s.sb("x", [R, T, D])
        xn = s.sb("xn", [R, T, D])
        stats = s.sb("stats", [R, T, 6])
        mv = s.sb("mv", [R, T, 2])
        rstd, var, root = (s.sb(n, [R, T]) for n in ("rstd", "var", "root"))
        gb = s.sb("gb", [128, 2, K])
        val = s.sb("val", [128, 2, K, R])
        tp = s.ps("tp", [128, 2, K, 128])
        x_in = [s.sem(f"x_in{j}") for j in range(T // 2)]
        gb_in = s.sem("gb_in")
        chain = s.sem("chain")
        moments = s.sem("moments")
        rooted = s.sem("rooted")
        normed = s.sem("normed")
        stored = s.sem("stored")
        turned = s.sem("turned")
        scaled = s.sem("scaled")
        fm_hi = s.sem("fm_hi")
        fm_ready = s.sem("fm_ready")
        block = s.block()
        affine = gain is not None
        last = xs if norms % 2 == 0 else xn
        at_end = norms * T

        @block.sync
        def _(sp):
            for j in range(T // 2):
                sp.dma_start(xs[:, 2 * j:2 * j + 2], x_dram[rows(j, 2 * R), :].rearrange("(t p) d -> p t d", p=R))\
                  .then_inc(x_in[j], 16)
            if affine:
                with nc.allow_non_contiguous_dma(reason="two short vectors"):
                    sp.dma_start(gb[:, 0], by_part(gain)).then_inc(gb_in, 16)
                    sp.dma_start(gb[:, 1], by_part(bias)).then_inc(gb_in, 16)
            if out_dram is not None:
                for j in range(T // 2):
                    sp.wait_ge(normed, 2 * j + 2)
                    sp.dma_start(out_dram[rows(j, 2 * R), :].rearrange("(t p) d -> p t d", p=R), xn[:, 2 * j:2 * j + 2])\
                      .then_inc(stored, 16)
                sp.wait_ge(stored, 16 * T // 2)

        @block.tensor
        def _(pe):
            for t in range(T):
                if norms:
                    pe.wait_ge(normed, at_end - T + t + 1)
                else:
                    pe.wait_ge(x_in[t // 2], 16)
                if t >= 2:
                    pe.wait_ge(fm_ready, t - 1)
                for k in range(K):
                    p = pe.transpose(tp[:, t % 2, k, 0:R], last[:, t, rows(k, 128)], c["ident"][0:R, 0:R])
                p.then_inc(turned, 1)

        @block.scalar
        def _(act):
            for n in range(norms):
                act.wait_ge(moments, n + 1)
                act.activation(root[:], var[:], ACT.Sqrt).then_inc(rooted, 1)
            for t in range(T):
                if affine:
                    act.wait_ge(scaled, t + 1)
                    act.activation(fm[:, 0, :, rows(t)], val[:, t % 2], ACT.Copy).then_inc(fm_hi, 1)
                else:
                    act.wait_ge(turned, t + 1)
                    act.activation(fm[:, 0, :, rows(t)], tp[:, t % 2, :, 0:R], ACT.Copy).then_inc(fm_hi, 1)

        @block.vector
        def _(dve):
            link = Chain(dve, chain)
            for n in range(norms):
                a, b = (xs, xn) if n % 2 == 0 else (xn, xs)
                if n:
                    dve.wait_ge(normed, n * T)
                row_moments(dve, link, a, stats, mv, (lambda t: dve.wait_ge(x_in[t // 2], 16)) if n == 0 else lambda t: None)
                link(dve.tensor_scalar(var[:], mv[:, :, 1], 1e-5, None, ALU.add))
                dve.sem_inc(moments, 1)
                dve.wait_ge(rooted, n + 1)
                inverse_root(dve, link, rstd[:], var[:], root[:])
                for t in range(T):
                    dve.tensor_scalar(b[:, t, :], a[:, t, :], mv[:, t, 0:1], rstd[:, t:t + 1],
                                      ALU.subtract, ALU.mult).then_inc(normed, 1)
            if affine:
                dve.wait_ge(gb_in, 32)
            for t in range(T):
                hi = fm[:, 0, :, rows(t)].bitcast(F32)
                if affine:
                    dve.wait_ge(turned, t + 1)
                    for k in range(K):
                        d = dve.tensor_scalar(val[:, t % 2, k, :], tp[:, t % 2, k, 0:R], gb[:, 0, k:k + 1],
                                              gb[:, 1, k:k + 1], ALU.mult, ALU.add)
                    d.then_inc(scaled, 1)
                dve.wait_ge(scaled if affine else fm_hi, t + 1)
                dve.wait_ge(fm_hi, t + 1)
                dve.tensor_tensor(fm[:, 1, :, rows(t)], val[:, t % 2] if affine else tp[:, t % 2, :, 0:R], hi,
                                  ALU.subtract).then_inc(fm_ready, 1)


VB = 12


def stage_heads(nc, c, fm, wq, wk, wv, bq, bk, bv, q2, k2, v2):
    with Stage(nc, "heads") as s:
        raw = s.sb("raw", [128, K, D])
        w = s.sb("w", [128, 2, K, D], F32R)
        bqk = s.sb("bqk", [128, 2, K])
        bvb = s.sb("bvb", [R, D])
        val = s.sb("val", [128, D])
        acc = s.ps("acc", [128, 4, D])
        raw_in = [s.sem(f"raw_in{i}") for i in range(3)]
        b_in = s.sem("b_in")
        w_hi = s.sem("w_hi")
        w_lo = s.sem("w_lo")
        done = s.sem("done")
        val_ready = s.sem("val_ready")
        hi_ready = s.sem("hi_ready")
        lo_ready = s.sem("lo_ready")
        block = s.block()
        NCH = len(CH)
        per = K * NCH
        units = [(i, m, ch) for i in range(2) for m in range(K) for ch in range(NCH)] + [(2, t, 0) for t in range(T)]
        first = (0, per, 2 * per, 2 * per + T)

        @block.sync
        def _(sp):
            with nc.allow_non_contiguous_dma(reason="two short vectors"):
                sp.dma_start(bqk[:, 0], by_part(bq)).then_inc(b_in, 16)
                sp.dma_start(bqk[:, 1], by_part(bk)).then_inc(b_in, 16)
            sp.dma_start(bvb[:], bv.partition_broadcast(R)).then_inc(b_in, 16)
            for i, ap in enumerate((wq, wk, wv)):
                if i:
                    sp.wait_ge(w_lo, i)
                sp.dma_start(raw[:], ap.rearrange("(k p) n -> p k n", p=128)).then_inc(raw_in[i], 16)

        @block.gpsimd
        def _(pool):
            for part in range(2):
                for blk in range(1, VB, 3):
                    pool.memset(v2[:, part, :, blk * 64:(blk + 1) * 64].bitcast(F32), 1.0 - part)
            for i in range(3):
                pool.wait_ge(raw_in[i], 16)
                if i:
                    pool.wait_ge(done, first[i])
                pool.tensor_copy(w[:, 0], raw[:]).then_inc(w_hi, 1)
            pool.drain()

        @block.tensor
        def _(pe):
            for u, (i, m, ch) in enumerate(units):
                if u == first[i]:
                    pe.wait_ge(w_lo, i + 1)
                if u >= 4:
                    pe.wait_ge(val_ready, u - 3)
                for k in range(K):
                    if i < 2:
                        c0, cn = CH[ch]
                        cols = rows(m, 128)
                        p = products3(pe, acc[:, u % 4, 0:cn], (w[:, 0, k, cols], w[:, 1, k, cols]),
                                      (fm[:, 0, k, c0:c0 + cn], fm[:, 1, k, c0:c0 + cn]), k == 0, k == K - 1)
                    else:
                        p = products3(pe, acc[0:R, u % 4, :], (fm[:, 0, k, rows(m)], fm[:, 1, k, rows(m)]),
                                      (w[:, 0, k, :], w[:, 1, k, :]), k == 0, k == K - 1)
                p.then_inc(done, 1)

        def place(u, part):
            i, m, ch = units[u]
            if i < 2:
                c0, cn = CH[ch]
                return (q2, k2)[i][:, part, m, c0:c0 + cn], val[:, 0:cn], acc[:, u % 4, 0:cn]
            pairs = lambda ap, n: ap.rearrange("p (g b c) -> p g b c", b=n, c=64)
            return (pairs(v2[:, part, m, :], 3)[:, :, 0:3:2, :], pairs(val[0:R, :], 2), pairs(acc[0:R, u % 4, :], 2))

        @block.scalar
        def _(act):
            for u in range(len(units)):
                dst, v, _ = place(u, 0)
                act.wait_ge(val_ready, u + 1)
                act.activation(dst, v, ACT.Copy).then_inc(hi_ready, 1)

        @block.vector
        def _(dve):
            def low(i):
                dve.wait_ge(w_hi, i + 1)
                dve.tensor_tensor(w[:, 1], raw[:], w[:, 0].bitcast(F32), ALU.subtract).then_inc(w_lo, 1)

            low(0)
            dve.wait_ge(b_in, 48)
            for u, (i, m, ch) in enumerate(units):
                if i and u == first[i]:
                    low(i)
                hi, v, a = place(u, 0)
                lo = place(u, 1)[0]
                dve.wait_ge(done, u + 1)
                if u:
                    dve.wait_ge(lo_ready, u)
                if i < 2:
                    d = dve.tensor_scalar(v, a, bqk[:, i, m:m + 1], (0.125, 1.0)[i], ALU.add, ALU.mult)
                else:
                    d = dve.tensor_tensor(v, a, bvb[:].rearrange("p (g b c) -> p g b c", b=2, c=64), ALU.add)
                d.then_inc(val_ready, 1)
                dve.wait_ge(val_ready, u + 1)
                dve.wait_ge(hi_ready, u + 1)
                dve.tensor_tensor(lo, v, hi.bitcast(F32), ALU.subtract).then_inc(lo_ready, 1)
            dve.wait_ge(lo_ready, len(units))


def stage_attend(nc, c, q2, k2, v2, at_dram, att):
    H = 8
    HALF = [(0, 314), (626, 312)]
    RB = 3
    with Stage(nc, "attend") as s:
        AT = s.sb("AT", [R, T, N], BF16)
        e = s.sb("e", [R, RB, 628])
        p2 = s.sb("p2", [R, 2, 2, 628], F32R)
        rz = s.sb("rz", [128, 2, 314])
        ob = s.sb("ob", [128, 2, 314])
        sp_ = s.ps("s", [R, RB, 2, 512])
        o = s.ps("o", [128, 2, 512])
        at_in = s.sem("at_in")
        s_done = s.sem("s_done")
        clipped = s.sem("clipped")
        exped = s.sem("exped")
        counted = s.sem("counted")
        p_hi = s.sem("p_hi")
        p_lo = s.sem("p_lo")
        pv_done = s.sem("pv_done")
        inverted = s.sem("inverted")
        o_used = s.sem("o_used")
        divided = s.sem("divided")
        block = s.block()
        units = [(h, half, st) for h in range(H) for half in range(2) for st in range(T)]
        NU = len(units)
        two = lambda ap, w: ap.rearrange("p (a n) -> p a n", a=2)

        def place(n):
            h, half, _ = units[n * T]
            mine, sums = (slice(0, 64), slice(64, 128)) if h % 2 == 0 else (slice(64, 128), slice(0, 64))
            return mine, sums, *HALF[half]

        @block.sync
        def _(sp):
            sp.dma_start(AT[:], at_dram).then_inc(at_in, 16)

        @block.tensor
        def _(pe):
            def scores(u):
                h, half, st = units[u]
                c0, w = HALF[half]
                part = slice(64 * (h % 2), 64 * (h % 2) + 64)
                if u >= RB:
                    pe.wait_ge(clipped, u - RB + 1)
                for a in range(2):
                    cols = slice(c0 + a * w, c0 + (a + 1) * w)
                    p = products3(pe, sp_[:, u % RB, a, 0:w], (k2[part, 0, h // 2, rows(st)], k2[part, 1, h // 2, rows(st)]),
                                  (q2[part, 0, h // 2, cols], q2[part, 1, h // 2, cols]), True, True)
                p.then_inc(s_done, 1)

            def values(u):
                h, half, st = units[u]
                w = HALF[half][1]
                blk = 64 * (3 * (h // 2) + h % 2)
                wh, wl = (v2[:, part, st, blk:blk + 128] for part in range(2))
                pe.wait_ge(p_lo, u + 1)
                if st == 0 and u:
                    pe.wait_ge(o_used, u // T)
                for a in range(2):
                    cols = slice(a * w, (a + 1) * w)
                    p = products3(pe, o[:, a, 0:w], (wh, wl), (p2[:, u % 2, 0, cols], p2[:, u % 2, 1, cols]),
                                  st == 0, st == T - 1)
                p.then_inc(pv_done, 1)

            for u in range(RB):
                scores(u)
            for u in range(NU):
                if u + RB < NU:
                    scores(u + RB)
                values(u)

        @block.vector
        def _(dve):
            def clip(u):
                w = HALF[units[u][1]][1]
                dve.wait_ge(s_done, u + 1)
                if u >= RB:
                    dve.wait_ge(p_lo, u - RB + 1)
                dve.tensor_scalar(two(e[:, u % RB, 0:2 * w], w), sp_[:, u % RB, :, 0:w], -5.0, 5.0, ALU.max, ALU.min)\
                   .then_inc(clipped, 1)

            def low(u):
                w = HALF[units[u][1]][1]
                dve.wait_ge(counted, u + 1)
                dve.wait_ge(p_hi, u + 1)
                if u >= 2:
                    dve.wait_ge(pv_done, u - 1)
                dve.tensor_tensor(p2[:, u % 2, 1, 0:2 * w], e[:, u % RB, 0:2 * w], p2[:, u % 2, 0, 0:2 * w].bitcast(F32),
                                  ALU.subtract).then_inc(p_lo, 1)

            def invert(n, a):
                mine, sums, _, w = place(n)
                dve.wait_ge(o_used, n + 1)
                if n:
                    dve.wait_ge(divided, n)
                dve.reciprocal(rz[mine, a, 0:w], ob[sums, a, 0:w]).then_inc(inverted, 1)

            for u in range(RB):
                clip(u)
            for u in range(NU):
                low(u)
                if u + RB < NU:
                    clip(u + RB)
                if u >= T and u % T in (0, 3):
                    invert(u // T - 1, (u % T) // 3)
            for a in range(2):
                invert(NU // T - 1, a)

        @block.scalar
        def _(act):
            def exp(u):
                w = HALF[units[u][1]][1]
                act.wait_ge(clipped, u + 1)
                act.activation(e[:, u % RB, 0:2 * w], e[:, u % RB, 0:2 * w], ACT.Exp).then_inc(exped, 1)

            for u in range(RB):
                exp(u)
            for u in range(NU):
                w = HALF[units[u][1]][1]
                act.wait_ge(counted, u + 1)
                if u >= 2:
                    act.wait_ge(pv_done, u - 1)
                act.activation(p2[:, u % 2, 0, 0:2 * w], e[:, u % RB, 0:2 * w], ACT.Copy).then_inc(p_hi, 1)
                if u + RB < NU:
                    exp(u + RB)
                if u % T == T - 1:
                    n = u // T
                    act.wait_ge(pv_done, u + 1)
                    if n:
                        act.wait_ge(divided, n)
                    act.activation(ob[:, :, 0:w], o[:, :, 0:w], ACT.Copy).then_inc(o_used, 1)

        @block.gpsimd
        def _(pool):
            def divide(n, u):
                mine, _, c0, w = place(n)
                pool.wait_ge(counted, u + 1)
                pool.wait_ge(inverted, 2 * (n + 1))
                h = units[n * T][0]
                pool.tensor_tensor(two(att[mine, h // 2, c0:c0 + 2 * w], w), ob[mine, :, 0:w], rz[mine, :, 0:w], ALU.mult)\
                    .then_inc(divided, 1)
                pool.wait_ge(divided, n + 1)

            pool.wait_ge(at_in, 16)
            for u, (h, half, st) in enumerate(units):
                c0, w = HALF[half]
                pool.wait_ge(exped, u + 1)
                pool.tensor_tensor(e[:, u % RB, 0:2 * w], e[:, u % RB, 0:2 * w], AT[:, st, c0:c0 + 2 * w], ALU.mult)\
                    .then_inc(counted, 1)
                if u >= T and u % T == T // 2:
                    divide(u // T - 1, u)
            divide(NU // T - 1, NU - 1)


def stage_att_out(nc, c, att, xn_dram, wo, bo, g1, b1, w1, bf1, w2, bf2, gn, bn, out):
    F = 2
    NCH = len(CH)
    with Stage(nc, "tail") as s:
        h1 = s.sb("h1", [R, T, D])
        ln = s.sb("ln", [R, T, D])
        a2 = s.sb("a2", [128, 2, K, N], F32R)
        f2 = s.sb("f2", [128, 2, F, N], F32R)
        raw = s.sb("raw", [128, K, D])
        w = s.sb("w", [128, 2, K, D], F32R)
        wf1_raw = raw[:].rearrange("p k n -> p (k n)")[:, 0:K * F * 128].rearrange("p (k n) -> p k n", k=K)
        wf2_raw = raw[:, K - F:K, :]
        wf1 = w[:].rearrange("p a k n -> p a (k n)")[:, :, 0:K * F * 128].rearrange("p a (k n) -> p a k n", k=K)
        wf2 = w[:, :, K - F:K, :]
        bob = s.sb("bob", [R, D])
        b2b = s.sb("b2b", [R, D])
        gnb = s.sb("gnb", [R, D])
        bnb = s.sb("bnb", [R, D])
        gb = s.sb("gb", [128, 2, K])
        bf = s.sb("bf", [128, F])
        val = s.sb("val", [128, 2, 512])
        stats = s.sb("stats", [R, T, 6])
        mv = s.sb("mv", [R, T, 2])
        rstd, var, root = (s.sb(n, [R, T]) for n in ("rstd", "var", "root"))
        acc = s.ps("acc", [128, 4, 512])
        tp = s.ps("tp", [128, 2, K, 128])
        x_in = s.sem("x_in")
        v_in = s.sem("v_in")
        raw_in = s.sem("raw_in")
        raw2_in = s.sem("raw2_in")
        w_hi = s.sem("w_hi")
        w_lo = s.sem("w_lo")
        att_hi = s.sem("att_hi")
        att_lo = s.sem("att_lo")
        chain = s.sem("chain")
        o_done = s.sem("o_done")
        h1_ready = s.sem("h1_ready")
        moments = s.sem("moments")
        rooted = s.sem("rooted")
        ln_ready = s.sem("ln_ready")
        turned = s.sem("turned")
        scaled = s.sem("scaled")
        l_hi = s.sem("l_hi")
        l_lo = s.sem("l_lo")
        f_done = s.sem("f_done")
        f_val = s.sem("f_val")
        f_hi = s.sem("f_hi")
        f_lo = s.sem("f_lo")
        y_done = s.sem("y_done")
        h2_ready = s.sem("h2_ready")
        out_ready = s.sem("out_ready")
        stored = s.sem("stored")
        block = s.block()
        FU = F * NCH
        view = lambda ap: ap.rearrange("(k p) n -> p k n", p=128)

        @block.sync
        def _(sp):
            sp.dma_start(raw[:], view(wo)).then_inc(raw_in, 16)
            sp.dma_start(h1[:], xn_dram.rearrange("(t p) d -> p t d", p=R)).then_inc(x_in, 16)
            for dst, v in ((bob, bo), (b2b, bf2), (gnb, gn), (bnb, bn)):
                sp.dma_start(dst[:], v.partition_broadcast(R)).then_inc(v_in, 16)
            with nc.allow_non_contiguous_dma(reason="short vectors"):
                sp.dma_start(gb[:, 0], by_part(g1)).then_inc(v_in, 16)
                sp.dma_start(gb[:, 1], by_part(b1)).then_inc(v_in, 16)
                sp.dma_start(bf[:], by_part(bf1)).then_inc(v_in, 16)
            sp.wait_ge(w_lo, 1)
            sp.dma_start(wf1_raw, view(w1)).then_inc(raw2_in, 16)
            sp.dma_start(wf2_raw, view(w2)).then_inc(raw2_in, 16)
            sp.wait_ge(out_ready, 2 * T)
            sp.dma_start(out.rearrange("(t p) d -> p t d", p=R), ln[:]).then_inc(stored, 16)
            sp.wait_ge(stored, 16)

        @block.gpsimd
        def _(pool):
            pool.wait_ge(raw_in, 16)
            pool.tensor_copy(w[:, 0], raw[:]).then_inc(w_hi, 1)
            pool.wait_ge(raw2_in, 32)
            pool.wait_ge(o_done, T)
            pool.tensor_copy(wf1[:, 0], wf1_raw)
            pool.tensor_copy(wf2[:, 0], wf2_raw).then_inc(w_hi, 1)
            pool.wait_ge(w_hi, 2)

        @block.tensor
        def _(pe):
            pe.wait_ge(w_lo, 1)
            for t in range(T):
                if t == 0:
                    pe.wait_ge(att_lo, K)
                if t >= 4:
                    pe.wait_ge(h1_ready, t - 3)
                for k in range(K):
                    p = products3(pe, acc[0:R, t % 4, :], (a2[:, 0, k, rows(t)], a2[:, 1, k, rows(t)]),
                                  (w[:, 0, k, :], w[:, 1, k, :]), k == 0, k == K - 1)
                p.then_inc(o_done, 1)
            for t in range(T):
                pe.wait_ge(ln_ready, t + 1)
                if t >= 2:
                    pe.wait_ge(scaled, t - 1)
                for k in range(K):
                    p = pe.transpose(tp[:, t % 2, k, 0:R], ln[:, t, rows(k, 128)], c["ident"][0:R, 0:R])
                p.then_inc(turned, 1)
            pe.wait_ge(w_lo, 3)
            pe.wait_ge(l_lo, T)
            for u in range(FU):
                m, (c0, cn) = u // NCH, CH[u % NCH]
                if u >= 4:
                    pe.wait_ge(f_val, u - 3)
                for k in range(K):
                    cols = rows(m, 128)
                    p = products3(pe, acc[:, u % 4, 0:cn], (wf1[:, 0, k, cols], wf1[:, 1, k, cols]),
                                  (a2[:, 0, k, c0:c0 + cn], a2[:, 1, k, c0:c0 + cn]), k == 0, k == K - 1)
                p.then_inc(f_done, 1)
            pe.wait_ge(f_lo, FU)
            for t in range(T):
                if t >= 4:
                    pe.wait_ge(h2_ready, t - 3)
                for k in range(F):
                    p = products3(pe, acc[0:R, t % 4, :], (f2[:, 0, k, rows(t)], f2[:, 1, k, rows(t)]),
                                  (wf2[:, 0, k, :], wf2[:, 1, k, :]), k == 0, k == F - 1)
                p.then_inc(y_done, 1)

        @block.scalar
        def _(act):
            for k in range(K):
                act.activation(a2[:, 0, k, :], att[:, k, :], ACT.Copy).then_inc(att_hi, 1)
            act.wait_ge(moments, 1)
            act.activation(root[:], var[:], ACT.Sqrt).then_inc(rooted, 1)
            for t in range(T):
                act.wait_ge(scaled, t + 1)
                act.activation(a2[:, 0, :, rows(t)], val[:, t % 2, 0:K * R].rearrange("p (k n) -> p k n", k=K),
                               ACT.Copy).then_inc(l_hi, 1)
            for u in range(FU):
                m, (c0, cn) = u // NCH, CH[u % NCH]
                act.wait_ge(f_done, u + 1)
                if u < 2:
                    act.wait_ge(l_lo, T)
                else:
                    act.wait_ge(f_lo, u - 1)
                act.activation(val[:, u % 2, 0:cn], acc[:, u % 4, 0:cn], ACT.Relu, bias=bf[:, m:m + 1]).then_inc(f_val, 1)
                act.wait_ge(f_val, u + 1)
                act.activation(f2[:, 0, m, c0:c0 + cn], val[:, u % 2, 0:cn], ACT.Copy).then_inc(f_hi, 1)
            act.wait_ge(moments, 2)
            act.activation(root[:], var[:], ACT.Sqrt).then_inc(rooted, 1)

        @block.vector
        def _(dve):
            link = Chain(dve, chain)

            def norm(n):
                row_moments(dve, link, h1, stats, mv)
                link(dve.tensor_scalar(var[:], mv[:, :, 1], 1e-5, None, ALU.add))
                dve.sem_inc(moments, 1)
                dve.wait_ge(rooted, n + 1)
                inverse_root(dve, link, rstd[:], var[:], root[:])
                for t in range(T):
                    dve.tensor_scalar(ln[:, t, :], h1[:, t, :], mv[:, t, 0:1], rstd[:, t:t + 1],
                                      ALU.subtract, ALU.mult).then_inc(ln_ready, 1)

            dve.wait_ge(w_hi, 1)
            dve.tensor_tensor(w[:, 1], raw[:], w[:, 0].bitcast(F32), ALU.subtract).then_inc(w_lo, 1)
            for k in range(K):
                dve.wait_ge(att_hi, k + 1)
                dve.tensor_tensor(a2[:, 1, k, :], att[:, k, :], a2[:, 0, k, :].bitcast(F32), ALU.subtract).then_inc(att_lo, 1)
            dve.wait_ge(x_in, 16)
            dve.wait_ge(v_in, 16 * 7)
            for t in range(T):
                d = dve.tensor_tensor(h1[:, t, :], h1[:, t, :], bob[:], ALU.add)
            link(d)
            for t in range(T):
                dve.wait_ge(o_done, t + 1)
                dve.tensor_tensor(h1[:, t, :], h1[:, t, :], acc[0:R, t % 4, :], ALU.add).then_inc(h1_ready, 1)
            dve.wait_ge(h1_ready, T)
            norm(0)
            for t in range(T):
                dve.wait_ge(turned, t + 1)
                if t >= 2:
                    dve.wait_ge(l_lo, t - 1)
                v = val[:, t % 2, 0:K * R].rearrange("p (k n) -> p k n", k=K)
                for k in range(K):
                    d = dve.tensor_scalar(v[:, k, :], tp[:, t % 2, k, 0:R], gb[:, 0, k:k + 1], gb[:, 1, k:k + 1],
                                          ALU.mult, ALU.add)
                d.then_inc(scaled, 1)
                dve.wait_ge(scaled, t + 1)
                dve.wait_ge(l_hi, t + 1)
                dve.tensor_tensor(a2[:, 1, :, rows(t)], v, a2[:, 0, :, rows(t)].bitcast(F32), ALU.subtract).then_inc(l_lo, 1)
            dve.wait_ge(w_hi, 2)
            dve.tensor_tensor(wf1[:, 1], wf1_raw, wf1[:, 0].bitcast(F32), ALU.subtract).then_inc(w_lo, 1)
            dve.tensor_tensor(wf2[:, 1], wf2_raw, wf2[:, 0].bitcast(F32), ALU.subtract).then_inc(w_lo, 1)
            for u in range(FU):
                m, (c0, cn) = u // NCH, CH[u % NCH]
                dve.wait_ge(f_hi, u + 1)
                dve.tensor_tensor(f2[:, 1, m, c0:c0 + cn], val[:, u % 2, 0:cn], f2[:, 0, m, c0:c0 + cn].bitcast(F32),
                                  ALU.subtract).then_inc(f_lo, 1)
            for t in range(T):
                d = dve.tensor_tensor(h1[:, t, :], h1[:, t, :], b2b[:], ALU.add)
            link(d)
            for t in range(T):
                dve.wait_ge(y_done, t + 1)
                dve.tensor_tensor(h1[:, t, :], h1[:, t, :], acc[0:R, t % 4, :], ALU.add).then_inc(h2_ready, 1)
            dve.wait_ge(h2_ready, T)
            norm(1)
            dve.wait_ge(ln_ready, 2 * T)
            for t in range(T):
                dve.tensor_tensor(ln[:, t, :], ln[:, t, :], gnb[:], ALU.mult).then_inc(out_ready, 1)
            dve.wait_ge(out_ready, T)
            for t in range(T):
                dve.tensor_tensor(ln[:, t, :], ln[:, t, :], bnb[:], ALU.add).then_inc(out_ready, 1)


VX = 66


def stage_qkv_biased(nc, c, fm, w_dram, b_dram, q, k_, vx):
    with Stage(nc, "qkvb") as s:
        raw = s.sb("raw", [128, 2, K, D])
        w = s.sb("w", [128, 2, K, D], F32R)
        bias = s.sb("bias", [R, 3, D])
        val = s.sb("val", [R, 2, D])
        acc = s.ps("acc", [R, 4, D])
        raw_in = [s.sem(f"raw_in{i}") for i in range(3)]
        b_in = s.sem("b_in")
        w_hi = s.sem("w_hi")
        w_lo = s.sem("w_lo")
        done = s.sem("done")
        used = s.sem("used")
        v_hi = s.sem("v_hi")
        v_lo = s.sem("v_lo")
        block = s.block()
        heads = lambda ap: ap.rearrange("p (h c) -> p h c", h=8)

        @block.sync
        def _(sp):
            sp.dma_start(bias[:].rearrange("p a n -> p (a n)"), b_dram.partition_broadcast(R)).then_inc(b_in, 16)
            for j in range(3):
                if j == 2:
                    sp.wait_ge(w_lo, 1)
                sp.dma_start(raw[:, j % 2], w_dram[:, rows(j, D)].rearrange("(k p) n -> p k n", p=128)).then_inc(raw_in[j], 16)

        @block.gpsimd
        def _(pool):
            for part in range(2):
                for h in range(8):
                    pool.memset(vx[:, part, :, h * VX + 64:(h + 1) * VX].bitcast(F32), 1.0 - part)
            for j in range(3):
                pool.wait_ge(raw_in[j], 16)
                if j:
                    pool.wait_ge(done, j * T)
                pool.tensor_copy(w[:, 0], raw[:, j % 2]).then_inc(w_hi, 1)
            pool.drain()

        @block.tensor
        def _(pe):
            for u in range(3 * T):
                j, t = u // T, u % T
                if t == 0:
                    pe.wait_ge(w_lo, j + 1)
                if u >= 4:
                    pe.wait_ge(used, u - 3)
                for k in range(K):
                    p = products3(pe, acc[:, u % 4, :], (fm[:, 0, k, rows(t)], fm[:, 1, k, rows(t)]),
                                  (w[:, 0, k, :], w[:, 1, k, :]), k == 0, k == K - 1)
                p.then_inc(done, 1)

        @block.scalar
        def _(act):
            for t in range(T):
                act.wait_ge(used, 2 * T + t + 1)
                act.activation(heads(vx[:, 0, t, :])[:, :, 0:64], heads(val[:, t % 2, :]), ACT.Copy).then_inc(v_hi, 1)

        @block.vector
        def _(dve):
            dve.wait_ge(b_in, 16)
            for u in range(3 * T):
                j, t = u // T, u % T
                if t == 0:
                    dve.wait_ge(w_hi, j + 1)
                    dve.tensor_tensor(w[:, 1], raw[:, j % 2], w[:, 0].bitcast(F32), ALU.subtract).then_inc(w_lo, 1)
                dve.wait_ge(done, u + 1)
                if j < 2:
                    dve.tensor_tensor((q, k_)[j][:, t, :], acc[:, u % 4, :], bias[:, j, :], ALU.add).then_inc(used, 1)
                    continue
                if t >= 2:
                    dve.wait_ge(v_lo, t - 1)
                dve.tensor_tensor(val[:, t % 2, :], acc[:, u % 4, :], bias[:, j, :], ALU.add).then_inc(used, 1)
                dve.wait_ge(used, u + 1)
                dve.wait_ge(v_hi, t + 1)
                dve.tensor_tensor(heads(vx[:, 1, t, :])[:, :, 0:64], heads(val[:, t % 2, :]),
                                  heads(vx[:, 0, t, :])[:, :, 0:64].bitcast(F32), ALU.subtract).then_inc(v_lo, 1)
            dve.wait_ge(v_lo, T)


def stage_features(nc, c, q, k_, vx, out):
    H, C = 8, 64
    ALPHA = 20.0
    PI = 3.141592653589793
    with Stage(nc, "feat") as s:
        tq = s.sb("tq", [R, T, D])
        tk = s.sb("tk", [R, T, D])
        sq = s.sb("sq", [R, 2, D])
        ss, nrm, inv, root = (s.sb(n, [R, 2, T, H]) for n in ("ss", "nrm", "inv", "root"))
        power = s.sb("power", [R, T, H])
        half_pi = s.sb("half_pi", [R, 1])
        cs = s.sb("cs", [R, 2, 2, D])
        f = s.sb("f", [R, 2, H, 2, C])
        f2 = s.sb("f2", [R, 2, 2, H, 2 * C], F32R)
        kv = s.sb("kv", [128, H, VX])
        kv2 = s.sb("kv2", [128, 2, H, VX], F32R)
        qT = s.sb("qT", [128, 2, 2, H, R], F32R)
        z = s.sb("z", [R, 2, H])
        o = s.sb("o", [R, 2, D])
        kvp = s.ps("kvp", [128, 2, 512])
        tp = s.ps("tp", [128, 2, 4, 128])
        op = s.ps("op", [R, 2, 2, 512])
        chain = s.sem("chain")
        squared = s.sem("squared")
        summed = s.sem("summed")
        rooted = s.sem("rooted")
        normal = s.sem("normal")
        qk_unit = s.sem("qk_unit")
        tanhed = s.sem("tanhed")
        powers = s.sem("powers")
        logs = s.sem("logs")
        scaled = s.sem("scaled")
        q_ready = s.sem("q_ready")
        k3_ready = s.sem("k3_ready")
        const = s.sem("const")
        cos_sin = s.sem("cos_sin")
        f_ready = s.sem("f_ready")
        f_hi = s.sem("f_hi")
        f_lo = s.sem("f_lo")
        kv_used = s.sem("kv_used")
        kv_hi = s.sem("kv_hi")
        kv_ready = s.sem("kv_ready")
        turned = s.sem("turned")
        t_hi = s.sem("t_hi")
        t_lo = s.sem("t_lo")
        o_done = s.sem("o_done")
        o_ready = s.sem("o_ready")
        stored = [s.sem(f"stored{b}") for b in range(2)]
        block = s.block()
        heads = lambda ap: ap.rearrange("p (h c) -> p h c", h=H)
        wide = lambda ap: ap.unsqueeze(2).to_broadcast([R, H, C])
        four = lambda ap: ap[:, 0:4 * VX].rearrange("p (h c) -> p h c", c=VX)

        @block.sync
        def _(sp):
            for t in range(T):
                sp.wait_ge(o_ready, t + 1)
                sp.dma_start(out[rows(t), :], o[:, t % 2, :]).then_inc(stored[t % 2], 16)
            for b in range(2):
                sp.wait_ge(stored[b], 16 * T // 2)

        @block.gpsimd
        def _(pool):
            pool.memset(half_pi[:], PI / 2).then_inc(const, 1)
            for n in range(2 * T):
                x = (q, k_)[n // T][:, n % T, :]
                if n >= 2:
                    pool.wait_ge(summed, n - 1)
                pool.tensor_tensor(sq[:, n % 2, :], x, x, ALU.mult).then_inc(squared, 1)

            def features(n):
                t, b = n % T, n % 2
                x = (k_, q)[n // T][:, t, :]
                if n == 0:
                    pool.wait_ge(k3_ready, T)
                if n == T:
                    pool.wait_ge(q_ready, T)
                if n >= 2:
                    pool.wait_ge(f_used(n - 2)[0], f_used(n - 2)[1])
                for i in range(2):
                    pool.wait_ge(cos_sin, 2 * n + i + 1)
                    pool.tensor_tensor(f[:, b, :, i, :], heads(x), heads(cs[:, b, i, :]), ALU.mult).then_inc(f_ready, 1)

            def f_used(n):
                return (f_lo, n + 1) if n < T else (turned, 2 * (n - T) + 2)

            for n in range(2 * T):
                features(n)
            pool.wait_ge(f_ready, 4 * T)

        @block.scalar
        def _(act):
            act.wait_ge(const, 1)
            act.wait_ge(normal, 1)
            act.activation(root[:], ss[:], ACT.Sqrt).then_inc(rooted, 1)
            act.wait_ge(normal, 2)
            act.activation(power[:], nrm[:, 0], ACT.Tanh).then_inc(tanhed, 1)
            for n in range(2 * T):
                act.wait_ge(qk_unit, n + 1)
                dst = (tq, tk)[n // T][:, n % T, :]
                act.activation(dst, dst, ACT.Tanh, scale=ALPHA).then_inc(tanhed, 1)

            def angles(n):
                t, b = n % T, n % 2
                x = (tk, tq)[n // T][:, t, :]
                if n >= 2:
                    act.wait_ge(f_ready, 2 * n - 2)
                act.activation(cs[:, b, 0, :], x, ACT.Sin, bias=half_pi[:], scale=-PI / 4).then_inc(cos_sin, 1)
                act.activation(cs[:, b, 1, :], x, ACT.Sin, scale=PI / 4).then_inc(cos_sin, 1)

            def high(n):
                act.wait_ge(f_ready, 2 * n + 2)
                if n >= 2:
                    act.wait_ge(kv_used, n - 1)
                act.activation(f2[:, n % 2, 0], f[:, n % 2].rearrange("p h i c -> p h (i c)"), ACT.Copy).then_inc(f_hi, 1)

            act.wait_ge(tanhed, 2 * T + 1)
            angles(0)
            for n in range(T):
                angles(n + 1)
                high(n)
            for t in range(T):
                act.wait_ge(powers, t + 1)
                act.activation(q[:, t, :], q[:, t, :], ACT.Ln).then_inc(logs, 1)
            for t in range(T):
                act.wait_ge(scaled, t + 1)
                act.activation(q[:, t, :], q[:, t, :], ACT.Exp).then_inc(q_ready, 1)
            act.wait_ge(kv_ready, 1)
            act.activation(kv2[:, 0], kv[:], ACT.Copy).then_inc(kv_hi, 1)
            for t in range(T):
                if t + 1 < T:
                    angles(T + t + 1)
                for g in range(2):
                    act.wait_ge(turned, 2 * t + g + 1)
                    if t >= 2:
                        act.wait_ge(o_done, t - 1)
                    act.activation(qT[:, t % 2, 0, 4 * g:4 * g + 4, :], tp[:, g, :, 0:R], ACT.Copy).then_inc(t_hi, 1)

        @block.vector
        def _(dve):
            link = Chain(dve, chain)
            for n in range(2 * T):
                dve.wait_ge(squared, n + 1)
                dve.tensor_reduce(ss[:, n // T, n % T, :], heads(sq[:, n % 2, :]), AX, ALU.add).then_inc(summed, 1)
            dve.wait_ge(summed, 2 * T)
            dve.sem_inc(normal, 1)
            dve.wait_ge(rooted, 1)
            inverse_root(dve, link, inv[:], ss[:], root[:])
            link(dve.tensor_tensor(nrm[:], ss[:], inv[:], ALU.mult))
            dve.sem_inc(normal, 1)
            for n in range(2 * T):
                i, t = n // T, n % T
                dve.tensor_tensor(heads((tq, tk)[i][:, t, :]), heads((q, k_)[i][:, t, :]), wide(inv[:, i, t, :]), ALU.mult)\
                   .then_inc(qk_unit, 1)
            dve.wait_ge(qk_unit, 2 * T)
            for t in range(T):
                if t:
                    dve.wait_ge(k3_ready, t)
                dve.tensor_tensor(sq[:, 0, :], k_[:, t, :], k_[:, t, :], ALU.mult)
                link(dve.scalar_tensor_tensor(out=sq[:, 1, :], in0=k_[:, t, :], scalar=-1.0, in1=k_[:, t, :],
                                              op0=ALU.mult, op1=ALU.max))
                dve.tensor_tensor(k_[:, t, :], sq[:, 1, :], sq[:, 0, :], ALU.mult).then_inc(k3_ready, 1)
            for t in range(T):
                link(dve.tensor_tensor(heads(q[:, t, :]), heads(q[:, t, :]), wide(inv[:, 0, t, :]), ALU.mult))
                link(dve.tensor_tensor(q[:, t, :], q[:, t, :], q[:, t, :], ALU.mult))
                dve.tensor_scalar(q[:, t, :], q[:, t, :], 1e-37, None, ALU.max).then_inc(powers, 1)
                dve.wait_ge(f_hi, t + 1)
                dve.tensor_tensor(f2[:, t % 2, 1], f[:, t % 2].rearrange("p h i c -> p h (i c)"),
                                  f2[:, t % 2, 0].bitcast(F32), ALU.subtract).then_inc(f_lo, 1)
            dve.wait_ge(tanhed, 1)
            link(dve.tensor_scalar(power[:], power[:], 1.5, 0.75, ALU.mult, ALU.add))
            for t in range(T):
                dve.wait_ge(logs, t + 1)
                dve.tensor_tensor(heads(q[:, t, :]), heads(q[:, t, :]), wide(power[:, t, :]), ALU.mult).then_inc(scaled, 1)
            dve.wait_ge(kv_used, T)
            for g in range(2):
                d = dve.tensor_scalar(kv[:, 4 * g:4 * g + 4, :], four(kvp[:, g, :]), 1.0 / N, None, ALU.mult)
            link(d)
            dve.sem_inc(kv_ready, 1)
            dve.wait_ge(kv_hi, 1)
            dve.tensor_tensor(kv2[:, 1], kv[:], kv2[:, 0].bitcast(F32), ALU.subtract).then_inc(kv_ready, 1)

            def low(t):
                for g in range(2):
                    dve.wait_ge(t_hi, 2 * t + g + 1)
                    dve.tensor_tensor(qT[:, t % 2, 1, 4 * g:4 * g + 4, :], tp[:, g, :, 0:R],
                                      qT[:, t % 2, 0, 4 * g:4 * g + 4, :].bitcast(F32), ALU.subtract).then_inc(t_lo, 1)

            low(0)
            for t in range(T):
                b = t % 2
                if t + 1 < T:
                    low(t + 1)
                dve.wait_ge(o_done, t + 1)
                if t >= 2:
                    dve.wait_ge(stored[b], 16 * (t // 2))
                for g in range(2):
                    d = dve.tensor_scalar(z[:, b, 4 * g:4 * g + 4], four(op[:, b, g, :])[:, :, 64], 1e-6, None, ALU.add)
                link(d)
                link(dve.reciprocal(z[:, b, :], z[:, b, :]))
                for g in range(2):
                    d = dve.tensor_tensor(heads(o[:, b, :])[:, 4 * g:4 * g + 4, :], four(op[:, b, g, :])[:, :, 0:64],
                                          z[:, b, 4 * g:4 * g + 4].unsqueeze(2).to_broadcast([R, 4, C]), ALU.mult)
                d.then_inc(o_ready, 1)

        @block.tensor
        def _(pe):
            for n in range(T):
                pe.wait_ge(f_lo, n + 1)
                for h in range(H):
                    wh, wl = (f2[:, n % 2, part, h, :] for part in range(2))
                    xh, xl = (vx[:, part, n, h * VX:(h + 1) * VX] for part in range(2))
                    dst = kvp[:, h // 4, (h % 4) * VX:(h % 4 + 1) * VX]
                    pe.matmul(dst, wh, xh, start=(n == 0 and h % 4 == 0), stop=False, skip_group_check=True)
                    pe.matmul(dst, wh, xl, start=False, stop=False, skip_group_check=True)
                    p = pe.matmul(dst, wl, xh, start=False, stop=(n == T - 1 and h % 4 == 3), skip_group_check=True)
                p.then_inc(kv_used, 1)

            def turn(t):
                n = T + t
                for g in range(2):
                    pe.wait_ge(f_ready, 2 * n + 2)
                    if t:
                        pe.wait_ge(t_lo, 2 * (t - 1) + g + 1)
                    for j in range(4):
                        p = pe.transpose(tp[:, g, j, 0:R], f[:, n % 2, 4 * g + j].rearrange("p i c -> p (i c)"),
                                         c["ident"][0:R, 0:R])
                    p.then_inc(turned, 1)

            turn(0)
            pe.wait_ge(kv_ready, 2)
            for t in range(T):
                b = t % 2
                if t + 1 < T:
                    turn(t + 1)
                pe.wait_ge(t_lo, 2 * t + 2)
                if t >= 2:
                    pe.wait_ge(o_ready, t - 1)
                for h in range(H):
                    p = products3(pe, op[:, b, h // 4, (h % 4) * VX:(h % 4 + 1) * VX],
                                  (qT[:, b, 0, h, :], qT[:, b, 1, h, :]), (kv2[:, 0, h, :], kv2[:, 1, h, :]), True, True)
                p.then_inc(o_done, 1)


def stage_rows_out(nc, c, name, fm, FK, w_dram, b_dram, out):
    with Stage(nc, name) as s:
        raw = s.sb("raw", [128, FK, D])
        w = s.sb("w", [128, 2, FK, D], F32R)
        bias = s.sb("bias", [R, D]) if b_dram is not None else None
        o = s.sb("o", [R, 2, D])
        acc = s.ps("acc", [R, 4, D])
        w_in = s.sem("w_in")
        w_hi = s.sem("w_hi")
        w_lo = s.sem("w_lo")
        done = s.sem("done")
        o_ready = s.sem("o_ready")
        stored = [s.sem(f"stored{b}") for b in range(2)]
        block = s.block()
        loads = 1 + (bias is not None)

        @block.sync
        def _(sp):
            sp.dma_start(raw[:], w_dram.rearrange("(k p) n -> p k n", p=128)).then_inc(w_in, 16)
            if bias is not None:
                sp.dma_start(bias[:], b_dram.partition_broadcast(R)).then_inc(w_in, 16)
            for t in range(T):
                sp.wait_ge(o_ready, t + 1)
                sp.dma_start(out[rows(t), :], o[:, t % 2, :]).then_inc(stored[t % 2], 16)
            for b in range(2):
                sp.wait_ge(stored[b], 16 * T // 2)

        @block.scalar
        def _(act):
            act.wait_ge(w_in, 16 * loads)
            act.activation(w[:, 0], raw[:], ACT.Copy).then_inc(w_hi, 1)

        @block.tensor
        def _(pe):
            pe.wait_ge(w_lo, 1)
            for t in range(T):
                if t >= 4:
                    pe.wait_ge(o_ready, t - 3)
                for k in range(FK):
                    p = products3(pe, acc[:, t % 4, :], (fm[:, 0, k, rows(t)], fm[:, 1, k, rows(t)]),
                                  (w[:, 0, k, :], w[:, 1, k, :]), k == 0, k == FK - 1)
                p.then_inc(done, 1)

        @block.vector
        def _(dve):
            dve.wait_ge(w_hi, 1)
            dve.tensor_tensor(w[:, 1], raw[:], w[:, 0].bitcast(F32), ALU.subtract).then_inc(w_lo, 1)
            for t in range(T):
                dve.wait_ge(done, t + 1)
                if t >= 2:
                    dve.wait_ge(stored[t % 2], 16 * (t // 2))
                if bias is None:
                    d = dve.tensor_copy(o[:, t % 2, :], acc[:, t % 4, :])
                else:
                    d = dve.tensor_tensor(o[:, t % 2, :], acc[:, t % 4, :], bias[:], ALU.add)
                d.then_inc(o_ready, 1)


def stage_gelu_hidden(nc, c, fm, w_dram, g2):
    F = 2
    NCH = len(CH)
    U = F * NCH
    with Stage(nc, "shid") as s:
        raw = s.sb("raw", [128, K, F * 128])
        w = s.sb("w", [128, 2, K, F * 128], F32R)
        val = s.sb("val", [128, 2, 418])
        acc = s.ps("acc", [128, 4, 512])
        w_in = s.sem("w_in")
        w_hi = s.sem("w_hi")
        w_lo = s.sem("w_lo")
        done = s.sem("done")
        val_ready = s.sem("val_ready")
        g_hi = s.sem("g_hi")
        g_lo = s.sem("g_lo")
        block = s.block()

        @block.sync
        def _(sp):
            sp.dma_start(raw[:], w_dram.rearrange("(k p) n -> p k n", p=128)).then_inc(w_in, 16)

        @block.tensor
        def _(pe):
            pe.wait_ge(w_lo, 1)
            for u in range(U):
                m, (c0, cn) = u // NCH, CH[u % NCH]
                if u >= 4:
                    pe.wait_ge(val_ready, u - 3)
                for k in range(K):
                    cols = rows(m, 128)
                    p = products3(pe, acc[:, u % 4, 0:cn], (w[:, 0, k, cols], w[:, 1, k, cols]),
                                  (fm[:, 0, k, c0:c0 + cn], fm[:, 1, k, c0:c0 + cn]), k == 0, k == K - 1)
                p.then_inc(done, 1)

        @block.scalar
        def _(act):
            act.wait_ge(w_in, 16)
            act.activation(w[:, 0], raw[:], ACT.Copy).then_inc(w_hi, 1)
            for u in range(U):
                m, (c0, cn) = u // NCH, CH[u % NCH]
                act.wait_ge(done, u + 1)
                if u >= 2:
                    act.wait_ge(g_lo, u - 1)
                act.activation(val[:, u % 2, 0:cn], acc[:, u % 4, 0:cn], ACT.Gelu).then_inc(val_ready, 1)
                act.wait_ge(val_ready, u + 1)
                act.activation(g2[:, 0, m, c0:c0 + cn], val[:, u % 2, 0:cn], ACT.Copy).then_inc(g_hi, 1)

        @block.vector
        def _(dve):
            dve.wait_ge(w_hi, 1)
            dve.tensor_tensor(w[:, 1], raw[:], w[:, 0].bitcast(F32), ALU.subtract).then_inc(w_lo, 1)
            for u in range(U):
                m, (c0, cn) = u // NCH, CH[u % NCH]
                dve.wait_ge(g_hi, u + 1)
                dve.tensor_tensor(g2[:, 1, m, c0:c0 + cn], val[:, u % 2, 0:cn], g2[:, 0, m, c0:c0 + cn].bitcast(F32),
                                  ALU.subtract).then_inc(g_lo, 1)
            dve.wait_ge(g_lo, U)


def build(nc, a, out):
    def dram(name, shape, dt=F32):
        return nc.dram_tensor(name, shape, dt).ap()

    x_mixed = dram("x_mixed", [N, D])
    h_dram = dram("h_dram", [LAYERS + 1, N, 3, D], BF16)
    wc_dram = dram("wc_dram", [LAYERS, 2, KC * 128, D])
    at_dram = dram("at_dram", [R, T, N], BF16)
    table_dram, flag_dram = dram("table_dram", [2, G]), dram("flag_dram", [R])
    x1, xn1, x2, xn2 = (dram(n, [N, D]) for n in ("x1", "xn1", "x2", "xn2"))
    gnn1, lin1, mix1 = (dram(n, [N, D]) for n in ("gnn1", "lin1", "mix1"))
    x3, xn3, shared = (dram(n, [N, D]) for n in ("x3", "xn3", "shared"))

    with ExitStack() as ctx:
        c = constants(nc, ctx)

        def sb(stack, name, shape, dt=F32, side=None):
            return stack.enter_context(nc.sbuf_tensor(name, shape, dt, side=side))

        right = ExitStack()
        with ExitStack() as left:
            fm = sb(left, "fm0", [128, 2, K, N], F32R)
            wq = sb(left, "wqkv0", [128, 2, K, 3 * D], F32R)
            rn = sb(left, "rn0", [R, T])
            stage_pre(nc, c, a["x"], a["L0_gnn_W_init"], a["L0_mix_w_qkv"], a["L0_mix_norm_w"], h_dram[0], fm, wq, rn)
            q = sb(right, "q0", [R, T, D], side="right")
            k = sb(right, "k0", [R, T, D], side="right")
            v2 = sb(right, "v0", [R, 2, T, D], F32R, side="right")
            stage_qkv(nc, c, fm, wq, rn, q, k, v2)
        stage_mix(nc, c, a["x"], q, k, v2, a["L0_mix_mem_fm"], a["L0_mix_mem_rows"], a["L0_mix_w_out"],
                  a["L0_mix_b_out"], a["L0_mix_out_norm_w"], x_mixed)
        right.close()

        stage_fuse(nc, c, a["L0_gnn_W_fwd"], a["L0_gnn_W_bwd"], a["L0_gnn_W_self"], wc_dram)
        with ExitStack() as left:
            A = sb(left, "A", [R, T, N], BF16)
            AT = sb(left, "AT", [R, T, N], BF16)
            stage_adjacency(nc, c, a["src"], a["dst"], a["dst_rows"], table_dram, flag_dram, A, AT)
            stage_gnn(nc, c, A, AT, at_dram, wc_dram, h_dram)

        def experts(layer, top, F, func, terms, gate, gate_b, w1, w3, w2, x_sum, xn, extra, dst):
            slots = max_passes(top) * CHUNK
            token_dram = dram(f"token{layer}", [slots + CHUNK, 1], I32)
            y_dram = dram(f"y{layer}", [slots, D])
            with ExitStack() as left:
                slot_i = sb(left, f"slot{layer}", [R, top, T], I32)
                weight = sb(left, f"weight{layer}", [R, top, T])
                table = sb(left, f"table{layer}", [1, 2, max_passes(top) + 1], I32)
                with ExitStack() as inner:
                    fm = sb(inner, f"fm_route{layer}", [128, 2, K, N], F32R)
                    stage_route(nc, c, f"route{layer}", terms, gate, gate_b, top, x_sum, xn, fm,
                                slot_i, weight, table, token_dram)
                    if extra is not None:
                        g2 = sb(inner, "hidden_shared", [128, 2, 2, N], F32R)
                        stage_gelu_hidden(nc, c, fm, a["L1_ffn_sw1"], g2)
                        stage_rows_out(nc, c, "shared", g2, 2, a["L1_ffn_sw2"], None, extra)
                stage_experts(nc, c, f"experts{layer}", top, F, func, w1, w3, w2, xn, token_dram, table, y_dram)
                stage_combine(nc, c, f"combine{layer}", top, x_sum, y_dram, slot_i, weight, extra, dst)

        experts(0, 2, a["L0_ffn_w1"].shape[2], ACT.Gelu, [x_mixed] + [h_dram[LAYERS, :, i, :] for i in range(3)],
                a["L0_ffn_wg"], a["L0_ffn_bg"], a["L0_ffn_w1"], a["L0_ffn_w3"], a["L0_ffn_w2"], x1, xn1, None, x2)

        g = {n: a["L1_gnn_" + n] for n in "Wq bq Wk bk Wv bv Wo bo g0 b0 g1 b1 W1 bf1 W2 bf2 gn bn".split()}
        right, left = ExitStack(), ExitStack()
        fm = sb(right, "fm1", [128, 2, K, N], F32R, side="right")
        stage_turn(nc, c, "turn1", x2, 2, xn2, g["g0"], g["b0"], fm)
        q2 = sb(left, "q1", [128, 2, K, N], F32R)
        k2 = sb(left, "k1", [128, 2, K, N], F32R)
        v2 = sb(left, "v1", [R, 2, T, VB * 64], F32R)
        stage_heads(nc, c, fm, g["Wq"], g["Wk"], g["Wv"], g["bq"], g["bk"], g["bv"], q2, k2, v2)
        right.close()
        right = ExitStack()
        att = sb(right, "att", [128, K, N], side="right")
        stage_attend(nc, c, q2, k2, v2, at_dram, att)
        left.close()
        stage_att_out(nc, c, att, xn2, g["Wo"], g["bo"], g["g1"], g["b1"], g["W1"], g["bf1"], g["W2"], g["bf2"],
                      g["gn"], g["bn"], gnn1)
        right.close()

        m = {n: a["L1_mix_" + n] for n in "qkv_w qkv_b ln_g ln_b out_w out_b".split()}
        right, left = ExitStack(), ExitStack()
        fm = sb(right, "fm2", [128, 2, K, N], F32R, side="right")
        stage_turn(nc, c, "turn2", xn2, 0, None, None, None, fm)
        q = sb(left, "q2", [R, T, D])
        k = sb(left, "k2", [R, T, D])
        vx = sb(left, "v2", [R, 2, T, 8 * VX], F32R)
        stage_qkv_biased(nc, c, fm, m["qkv_w"], m["qkv_b"], q, k, vx)
        right.close()
        stage_features(nc, c, q, k, vx, lin1)
        left.close()
        with ExitStack() as left:
            fm = sb(left, "fm3", [128, 2, K, N], F32R)
            stage_turn(nc, c, "turn3", lin1, 1, None, m["ln_g"], m["ln_b"], fm)
            stage_rows_out(nc, c, "mix_out", fm, K, m["out_w"], m["out_b"], mix1)

        experts(1, 1, a["L1_ffn_w1"].shape[2], ACT.Silu, [x2, gnn1, mix1], a["L1_ffn_gate_w"], None,
                a["L1_ffn_w1"], a["L1_ffn_w3"], a["L1_ffn_w2"], x3, xn3, shared, out)


def kernel(**inputs):
    import numpy as _np
    import concourse.bacc as _bacc
    from concourse.bass_utils import run_bass_kernel_spmd as _run

    a = {name: _np.asarray(value) for name, value in inputs.items()}

    def turned(name):
        a[name] = a[name].swapaxes(-1, -2)

    for name in ("L0_gnn_W_init", "L0_gnn_W_self", "L1_ffn_gate_w", "L1_ffn_w1", "L1_ffn_w3", "L1_ffn_w2",
                 "L1_ffn_sw1", "L1_ffn_sw2"):
        turned(name)
    a["dst_rows"] = a["dst"].reshape(G, EG * R)
    for name in ("src", "dst"):
        a[name] = a[name].reshape(G, R, EG).transpose(1, 0, 2).reshape(R, G * EG)
    a["L0_mix_norm_w"] = a["L0_mix_norm_w"].reshape(K, 128).T
    a["L0_mix_out_norm_w"] = a["L0_mix_out_norm_w"].reshape(D)
    mem = a.pop("L0_mix_mem_kv").reshape(2, D, 8)
    a["L0_mix_mem_fm"] = mem[0]
    a["L0_mix_mem_rows"] = mem.transpose(0, 2, 1)

    nc = _bacc.Bacc("TRN2", target_bir_lowering=False, num_devices=1)
    arrays = {name: _np.ascontiguousarray(value) for name, value in a.items()}
    aps = {name: nc.dram_tensor(name, list(v.shape), mybir.dt.from_np(v.dtype), kind="ExternalInput").ap()
           for name, v in arrays.items()}
    out = nc.dram_tensor("out", [N, D], F32, kind="ExternalOutput").ap()
    build(nc, aps, out)
    r = _run(nc, [arrays], core_ids=[0])
    return r.results[0]["out"]
```
